# Optimizing a Trainium2 kernel written in Bass

```python
import numpy as np
import jax
import jax.numpy as jnp

def _softmax(x, axis=-1):
    return jax.nn.softmax(x, axis=axis)

def _gelu(x):
    return jax.nn.gelu(x, approximate=True)

def _silu(x):
    return jax.nn.silu(x)

def _sigmoid(x):
    return jax.nn.sigmoid(x)

def _layernorm(x, axis=-1, eps=1e-05):
    m = jnp.mean(x, axis=axis, keepdims=True)
    v = jnp.var(x, axis=axis, keepdims=True)
    return (x - m) / jnp.sqrt(v + eps)

def _scatter_add(tgt, idx, src, axis=0):
    return tgt.at[idx].add(src)

def _segment_sum(src, seg, n):
    return jax.ops.segment_sum(src, seg, n)
kernel_name = 'mk_hybrid_d1_jaxref_r4_891d67'

def setup_inputs(seed: int=0):
    np.random.seed(seed)
    _w = jnp.asarray

    def _L0_attn_a_setup():
        import jax, jax.numpy as jnp
        import numpy as np
        from math import log2, floor
        HEADS = 16
        DIM_HEAD = 64
        SCALE = DIM_HEAD ** (-0.5)

        def _get_slopes(heads):

            def pow2_slopes(n):
                start = 2 ** (-2 ** (-(log2(n) - 3)))
                return [start * start ** i for i in range(n)]
            if log2(heads).is_integer():
                return pow2_slopes(heads)
            c = 2 ** floor(log2(heads))
            return pow2_slopes(c) + pow2_slopes(2 * c)[0::2][:heads - c]
        key = jax.random.key(seed)
        k1, k2, k3 = jax.random.split(key, 3)
        b, n, dim = (2, 512, 256)
        inner = HEADS * DIM_HEAD
        x = jax.random.normal(k1, (b, n, dim), dtype=jnp.float32)
        w_qkv = jax.random.normal(k2, (dim, 3 * inner), dtype=jnp.float32) * dim ** (-0.5)
        w_out = jax.random.normal(k3, (inner, dim), dtype=jnp.float32) * inner ** (-0.5)
        b_out = jnp.zeros((dim,), dtype=jnp.float32)
        return {'x': x, 'w_qkv': w_qkv, 'w_out': w_out, 'b_out': b_out}
    _L0_attn_a_in = _L0_attn_a_setup()

    def _L0_attn_b_setup():
        import jax, jax.numpy as jnp
        import numpy as np
        INF_APPROX = 1e+30
        ROTARY_BASE = 10000.0
        D_HEAD = 128

        def _rope(x, base=ROTARY_BASE):
            _, length, _, width = x.shape
            half = width // 2
            positions = jnp.arange(length, dtype=x.dtype)
            dims = jnp.arange(half, dtype=x.dtype)
            ang_freqs = jnp.power(base, -dims / half)
            radians = positions[:, None] * ang_freqs[None, :]
            cos = jnp.cos(radians)[None, :, None, :]
            sin = jnp.sin(radians)[None, :, None, :]
            even, odd = jnp.split(x, 2, axis=-1)
            return jnp.concatenate([even * cos - odd * sin, even * sin + odd * cos], axis=-1)
        key = jax.random.key(seed)
        k1, k2, k3, k4, k5 = jax.random.split(key, 5)
        B, T, M, H, D = (2, 1024, 256, 8, 128)
        n_layer = 24
        x = jax.random.normal(k1, (B, T, M), dtype=jnp.float32)
        std_qkv = M ** (-0.5)
        std_o = (M * 2 * n_layer) ** (-0.5)
        w_aq = jnp.zeros((M, H, D), dtype=jnp.float32)
        w_ak = std_qkv * jax.random.normal(k3, (M, H, D), dtype=jnp.float32)
        w_av = std_qkv * jax.random.normal(k4, (M, H, D), dtype=jnp.float32)
        w_ao = std_o * jax.random.normal(k5, (H, D, M), dtype=jnp.float32)
        return {'x': x, 'w_aq': w_aq, 'w_ak': w_ak, 'w_av': w_av, 'w_ao': w_ao}
    _L0_attn_b_in = _L0_attn_b_setup()

    def _L0_ffn_setup():
        import jax, jax.numpy as jnp
        import numpy as np
        B, S, D = (2, 256, 256)
        E, K, I = (8, 2, 256)
        LIMIT = 7.0
        ALPHA = 1.702

        def _swiglu(t, limit):
            glu = jnp.minimum(t[..., ::2], limit)
            lin = jnp.clip(t[..., 1::2], -limit, limit)
            return glu * jax.nn.sigmoid(ALPHA * glu) * (lin + 1.0)
        key = jax.random.key(seed)
        k0, k1, k2, k3 = jax.random.split(key, 4)
        return {'x': jax.random.normal(k0, (B, S, D), jnp.float32), 'norm_w': jnp.ones((D,), jnp.float32), 'gate_w': jax.random.normal(k1, (E, D), jnp.float32) / np.sqrt(D).astype(np.float32), 'gate_b': jnp.zeros((E,), jnp.float32), 'mlp1_w': jax.random.normal(k2, (E, 2 * I, D), jnp.float32) / np.sqrt(D).astype(np.float32), 'mlp1_b': jnp.zeros((E, 2 * I), jnp.float32), 'mlp2_w': jax.random.normal(k3, (E, D, I), jnp.float32) / np.sqrt(I).astype(np.float32), 'mlp2_b': jnp.zeros((E, D), jnp.float32)}
    _L0_ffn_in = _L0_ffn_setup()
    _d = {'L0_attn_a_x': _L0_attn_a_in['x'], 'L0_attn_a_w_qkv': _L0_attn_a_in['w_qkv'], 'L0_attn_a_w_out': _L0_attn_a_in['w_out'], 'L0_attn_a_b_out': _L0_attn_a_in['b_out'], 'L0_attn_b_w_aq': _L0_attn_b_in['w_aq'], 'L0_attn_b_w_ak': _L0_attn_b_in['w_ak'], 'L0_attn_b_w_av': _L0_attn_b_in['w_av'], 'L0_attn_b_w_ao': _L0_attn_b_in['w_ao'], 'L0_ffn_norm_w': _L0_ffn_in['norm_w'], 'L0_ffn_gate_w': _L0_ffn_in['gate_w'], 'L0_ffn_gate_b': _L0_ffn_in['gate_b'], 'L0_ffn_mlp1_w': _L0_ffn_in['mlp1_w'], 'L0_ffn_mlp1_b': _L0_ffn_in['mlp1_b'], 'L0_ffn_mlp2_w': _L0_ffn_in['mlp2_w'], 'L0_ffn_mlp2_b': _L0_ffn_in['mlp2_b']}
    _x0 = _d['L0_attn_a_x']
    _d['L0_attn_a_x'] = jax.random.normal(jax.random.fold_in(jax.random.key(seed), 1), (8, 512, 256), dtype=_x0.dtype)
    del _x0
    return _d

def reference(L0_attn_a_x, L0_attn_a_w_qkv, L0_attn_a_w_out, L0_attn_a_b_out, L0_attn_b_w_aq, L0_attn_b_w_ak, L0_attn_b_w_av, L0_attn_b_w_ao, L0_ffn_norm_w, L0_ffn_gate_w, L0_ffn_gate_b, L0_ffn_mlp1_w, L0_ffn_mlp1_b, L0_ffn_mlp2_w, L0_ffn_mlp2_b):

    def _L0_attn_a_ref(x, w_qkv, w_out, b_out):
        import jax, jax.numpy as jnp
        import numpy as np
        from math import log2, floor
        HEADS = 16
        DIM_HEAD = 64
        SCALE = DIM_HEAD ** (-0.5)

        def _get_slopes(heads):

            def pow2_slopes(n):
                start = 2 ** (-2 ** (-(log2(n) - 3)))
                return [start * start ** i for i in range(n)]
            if log2(heads).is_integer():
                return pow2_slopes(heads)
            c = 2 ** floor(log2(heads))
            return pow2_slopes(c) + pow2_slopes(2 * c)[0::2][:heads - c]
        b, n, _ = x.shape
        qkv = x @ w_qkv
        q, k, v = jnp.split(qkv, 3, axis=-1)

        def to_heads(t):
            return t.reshape(b, n, HEADS, DIM_HEAD).transpose(0, 2, 1, 3)
        q, k, v = map(to_heads, (q, k, v))
        q = q * SCALE
        sim = jnp.einsum('bhid,bhjd->bhij', q, k)
        slopes = jnp.asarray(_get_slopes(HEADS), dtype=sim.dtype)[:, None, None]
        i = jnp.arange(n)
        rel = -jnp.abs(i[None, :] - i[:, None]).astype(sim.dtype)
        sim = sim + rel[None, :, :] * slopes
        causal = jnp.triu(jnp.ones((n, n), dtype=bool), 1)
        mask_value = -jnp.finfo(sim.dtype).max
        sim = jnp.where(causal, mask_value, sim)
        attn = jax.nn.softmax(sim, axis=-1)
        out = jnp.einsum('bhij,bhjd->bhid', attn, v)
        out = out.transpose(0, 2, 1, 3).reshape(b, n, HEADS * DIM_HEAD)
        return out @ w_out + b_out

    def _L0_attn_b_ref(x, w_aq, w_ak, w_av, w_ao):
        import jax, jax.numpy as jnp
        import numpy as np
        INF_APPROX = 1e+30
        ROTARY_BASE = 10000.0
        D_HEAD = 128

        def _rope(x, base=ROTARY_BASE):
            _, length, _, width = x.shape
            half = width // 2
            positions = jnp.arange(length, dtype=x.dtype)
            dims = jnp.arange(half, dtype=x.dtype)
            ang_freqs = jnp.power(base, -dims / half)
            radians = positions[:, None] * ang_freqs[None, :]
            cos = jnp.cos(radians)[None, :, None, :]
            sin = jnp.sin(radians)[None, :, None, :]
            even, odd = jnp.split(x, 2, axis=-1)
            return jnp.concatenate([even * cos - odd * sin, even * sin + odd * cos], axis=-1)
        B, T, M = x.shape
        q = jnp.einsum('btm,mhd->bthd', x, w_aq)
        k = jnp.einsum('btm,mhd->bthd', x, w_ak)
        v = jnp.einsum('btm,mhd->bthd', x, w_av)
        q = _rope(q)
        k = _rope(k)
        s = jnp.einsum('bihd,bjhd->bhij', q, k) / D_HEAD
        i = jnp.arange(T)[:, None]
        j = jnp.arange(T)[None, :]
        mask = (i < j).astype(x.dtype)[None, None, :, :]
        s = s - jnp.asarray(INF_APPROX, x.dtype) * mask
        p = jax.nn.softmax(s, axis=-1)
        o = jnp.einsum('bhij,bjhd->bihd', p, v)
        r = jnp.einsum('bihd,hdm->bim', o, w_ao)
        return r

    def _L0_ffn_ref(x, norm_w, gate_w, gate_b, mlp1_w, mlp1_b, mlp2_w, mlp2_b):
        import jax, jax.numpy as jnp
        import numpy as np
        B, S, D = (2, 256, 256)
        E, K, I = (8, 2, 256)
        LIMIT = 7.0
        ALPHA = 1.702

        def _swiglu(t, limit):
            glu = jnp.minimum(t[..., ::2], limit)
            lin = jnp.clip(t[..., 1::2], -limit, limit)
            return glu * jax.nn.sigmoid(ALPHA * glu) * (lin + 1.0)
        eps = jnp.finfo(x.dtype).eps
        h = x * jax.lax.rsqrt(jnp.mean(x * x, axis=-1, keepdims=True) + eps) * norm_w
        flat = h.reshape(-1, D)
        logits = flat @ gate_w.T + gate_b
        vals, idx = jax.lax.top_k(logits, K)
        wts = jax.nn.softmax(vals, axis=-1)
        t1 = jnp.einsum('td,efd->tef', flat, mlp1_w) + mlp1_b
        act = _swiglu(t1, LIMIT)
        y = jnp.einsum('tei,edi->ted', act, mlp2_w) + mlp2_b
        sel = jnp.take_along_axis(y, idx[:, :, None], axis=1)
        out = jnp.sum(sel * wts[:, :, None], axis=1).reshape(x.shape)
        return x + out
    x = L0_attn_a_x
    x = x + _L0_attn_a_ref(_layernorm(x, axis=-1), L0_attn_a_w_qkv, L0_attn_a_w_out, L0_attn_a_b_out)
    x = x + _L0_ffn_ref(_layernorm(x, axis=-1), L0_ffn_norm_w, L0_ffn_gate_w, L0_ffn_gate_b, L0_ffn_mlp1_w, L0_ffn_mlp1_b, L0_ffn_mlp2_w, L0_ffn_mlp2_b)
    x = x + _L0_attn_b_ref(_layernorm(x, axis=-1), L0_attn_b_w_aq, L0_attn_b_w_ak, L0_attn_b_w_av, L0_attn_b_w_ao)
    x = x + _L0_ffn_ref(_layernorm(x, axis=-1), L0_ffn_norm_w, L0_ffn_gate_w, L0_ffn_gate_b, L0_ffn_mlp1_w, L0_ffn_mlp1_b, L0_ffn_mlp2_w, L0_ffn_mlp2_b)
    return x

_drawn_inputs = setup_inputs


def setup_inputs(seed=0):
    import zlib

    import numpy as np

    out = dict(_drawn_inputs(seed))
    spreads = {'L0_attn_a_b_out': (0.0, 0.1),
     'L0_attn_b_w_aq': (0.0, 0.8),
     'L0_ffn_norm_w': (1.0, 0.2),
     'L0_ffn_gate_b': (0.0, 0.1),
     'L0_ffn_mlp1_b': (0.0, 0.1),
     'L0_ffn_mlp2_b': (0.0, 0.1)}
    factors = {'L0_attn_b_w_ak': 8.0}
    for name, (base, spread) in spreads.items():
        noise = np.random.default_rng([zlib.crc32(name.encode()), seed]).standard_normal(out[name].shape)
        drawn = base * np.exp(spread * noise) if base else spread * noise
        out[name] = jnp.asarray(drawn.astype(out[name].dtype))
    for name, factor in factors.items():
        out[name] = (out[name] * factor).astype(out[name].dtype)
    return out
```

```python
from contextlib import ExitStack
from math import log2

import numpy as np

import concourse.bass as bass
from concourse import mybir

F32 = mybir.dt.float32
F32R = mybir.dt.float32r
I32 = mybir.dt.int32
U32 = mybir.dt.uint32
ALU = mybir.AluOpType
ACT = mybir.ActivationFunctionType
AX = mybir.AxisListType.X

NB, N, D = 8, 512, 256
TT = N // 128
NT = NB * TT
E, HID = 8, 256
NS = 2 * NT + E - 1
NSP = 72
WIDE = 1280
OFF = [0, 128, 384, 768]
PTO = [0, 512, 1024, 896]
LIMIT, ALPHA = 7.0, 1.702

C_ID, C_IOTA, C_TRI, C_P, C_TOK, C_I8 = 0, 128, 256, 384, 385, 417
C_N = 432


class Sem:

    def __init__(self, h, step):
        self.h, self.step, self.n = h, step, 0

    def tick(self):
        self.n += self.step
        return (self, self.n)


class Queue:

    def __init__(self):
        self.items, self.waited = [], {}

    def wait(self, *tokens):
        for t in tokens:
            if t is None:
                continue
            if isinstance(t, list):
                self.wait(*t)
                continue
            s, v = t
            if self.waited.get(id(s), 0) < v:
                self.waited[id(s)] = v
                self.items.append(lambda e, s=s, v=v: e.wait_ge(s.h, v))

    def go(self, fn, *tokens, sig=None):
        self.wait(*tokens)
        if sig is None:
            self.items.append(fn)
            return None
        t = sig.tick()
        self.items.append(lambda e: fn(e).then_inc(sig.h, sig.step))
        return t

    def play(self, e):
        for f in self.items:
            f(e)


def program(nc, T):
    ctx = ExitStack()
    PE, AC, DV, PO, SP = Queue(), Queue(), Queue(), Queue(), Queue()
    sems = {}

    def S(name, step=1):
        if name not in sems:
            sems[name] = Sem(ctx.enter_context(nc.semaphore(name)), step)
        return sems[name]

    def dma(dst, src, name, *tokens):
        return SP.go(lambda e: e.dma_start(dst, src), *tokens, sig=S(name, 16))

    def dram(name, shape):
        return nc.dram_tensor(name, shape, F32).ap()

    with ctx:
        def sb(name, shape, dt=F32, c=ctx):
            return c.enter_context(nc.sbuf_tensor(name, shape, dt))

        bank = [ctx.enter_context(nc.psum_tensor(f"bank{i}", [128, 512], F32)) for i in range(8)]
        hD = [dram(f"hD{i}", [NT * 128, D]) for i in range(2)]
        rD = [dram(f"rD{i}", [NT * 128, D]) for i in range(2)]
        yD = [dram(f"yD{i}", [NS * 128, D]) for i in range(2)]

        cst = sb("cst", [128, C_N])
        ident = cst[:, C_ID:C_ID + 128]
        bout = sb("bout", [128, D])
        nw = sb("nw", [128, D])
        gw = sb("gw", [128, 2, E])
        gb = sb("gb", [128, E])
        mhalf = sb("mhalf", [128, TT])
        stage = sb("stage", [128, 2, 512])
        Wh = sb("Wh", [128, 2, 3072], F32R)
        Wl = sb("Wl", [128, 2, 3072], F32R)
        WO = sb("WO", [128, 8, D])
        M1 = sb("M1", [128, NT, E])
        M2 = sb("M2", [128, NT, E])
        w1 = sb("w1", [128, NT])
        w2 = sb("w2", [128, NT])
        dI = sb("dI", [128, 2, NT], I32)
        idx = sb("idx", [128, NSP], I32)
        etab = sb("etab", [1, NSP], I32)

        t_cst = [dma(cst[:], T["c_cst"], "d_cst"), dma(bout[:], T["b_out"].partition_broadcast(128), "d_cst"),
                 dma(nw[:], T["norm_w"].partition_broadcast(128), "d_cst"),
                 dma(gw[:], T["gate_wT"], "d_cst"), dma(gb[:], T["gate_b"].partition_broadcast(128), "d_cst")]
        t_cst = t_cst[-1]
        t_mh = DV.go(lambda e: e.memset(mhalf[:], -0.5), sig=S("v_mh"))
        for q in (PE, AC, DV, PO):
            q.wait(t_cst)
        PO.wait(t_mh)

        st_free = [None, None]
        st_n = [0]

        def split_load(pieces, extra=None):
            done = []
            n = 512
            for src, hi, lo in [(a[:, i:i + n], b[:, i:i + n], c[:, i:i + n])
                                for a, b, c in pieces for i in range(0, 1024, n)]:
                k = st_n[0] % 2
                st_n[0] += 1
                t = dma(stage[:, k, 0:n], src, f"d_stage{k}", st_free[k])
                a = AC.go(lambda e, k=k, hi=hi, n=n: e.copy(hi, stage[:, k, 0:n]), t, extra, sig=S("a_whi"))
                b = DV.go(lambda e, k=k, hi=hi, lo=lo, n=n: e.tensor_tensor(
                    lo, stage[:, k, 0:n], hi.bitcast(F32), ALU.subtract), a, t, extra, sig=S("v_wlo"))
                st_free[k] = [a, b]
                done = [a, b]
            return done

        def load_attention(ph, extra=None):
            src = T["qkv"][ph]
            pieces = [(src[:, kc, j * 1024:(j + 1) * 1024], Wh[:, kc, j * 1024:(j + 1) * 1024],
                       Wl[:, kc, j * 1024:(j + 1) * 1024]) for j in range(3) for kc in range(2)]
            done = split_load(pieces, extra)
            return done + [dma(WO[:], T["wo"][ph], "d_wo", extra)]

        def attention(ph, t_w, start, t_prev):
            A = ph == 0
            HU = 2 if A else 1
            KD = 64 if A else 128
            NU = NB * 8
            c = ExitStack()

            def b(name, shape, dt=F32):
                return sb(f"{name}_{ph}", shape, dt, c)

            with c:
                tab = b("tab", [128, 16, 512]) if A else b("tab", [128, 3, 512])
                X = b("X", [128, 2, TT, D])
                xn = b("xn", [128, TT, D])
                xTh = b("xTh", [128, 2, 512], F32R)
                xTl = b("xTl", [128, 2, 512], F32R)
                Qh, Ql, Kh, Kl = (b(f"q{i}", [128, 2, 512], F32R) for i in range(4))
                V = b("V", [128, 2, TT, 512])
                NP = 3 if A else 2
                P = b("P", [128, NP, WIDE])
                PT = b("PT", [128, 2, WIDE])
                OT = b("OT", [128, 8, 512])
                mx = b("mx", [128, NP, 4])
                nm = b("nm", [128, NP, 4])
                rs = b("rs", [128, NP, 4])
                rc = b("rc", [128, NP, 4])
                st = b("st", [128, TT, 6])
                mv = b("mv", [128, TT, 2])
                ve = b("ve", [128, TT])
                rstd = b("rstd", [128, TT])
                xs = b("xs", [128, TT, D])
                hh = b("hh", [128, TT, D])
                hT = b("hT", [128, 2, 512])
                ss = b("ss", [128, TT])
                r2 = b("r2", [128, TT])
                lg = b("lg", [128, TT, E])
                v8 = b("v8", [128, TT, E])
                i8 = b("i8", [128, TT, E], U32)
                if8 = b("if8", [128, TT, E])
                dv = b("dv", [128, TT])
                if not A:
                    rp = b("rp", [128, 2, 2, 512])
                    rf = b("rf", [128, 2, 512])
                    yg = b("yg", [128, 2, 2, D])

                t_tab = [dma(tab[:], T["tab"][ph], "d_tab", start)]
                if start:
                    for q in (PE, AC, DV, PO):
                        q.wait(start)

                t_x, t_xT, xT_used = {}, {}, [None]
                t_q, t_v, qk_used, v_used = {}, {}, {}, {}
                p_ready, p_exp, p_used = {}, {}, {}
                pt_ready, pt_used, ot_used = {}, {}, {}
                bank_free = {i: None for i in range(8)}
                t_y, t_xpre = {}, {}
                B_Q, B_S, B_T, B_O, B_M = (0, 1), (2, 3), (4, 5), 6, 7
                cnt = {"s": 0, "t": 0, "m": 0, "yg": 0}
                yg_free = [None, None]

                def load_x(bt):
                    k = bt % 2
                    free = t_y.get(bt - 2)
                    if A:
                        t_x[bt] = dma(X[:, k], T["x"][bt].rearrange("(t p) d -> p t d", p=128), f"d_x{k}", free)
                        return
                    prev = rD[0].rearrange("(b t p) d -> b p t d", p=128, t=TT)
                    tx = dma(X[:, k], prev[bt], f"d_x{k}", free)
                    for t in range(TT):
                        g = bt * TT + t
                        s = cnt["yg"] % 2
                        cnt["yg"] += 1
                        ty = None
                        for j in range(2):
                            ty = PO.go(lambda e, s=s, j=j, g=g: e.indirect_dma_start(
                                yg[:, s, j, :], None, yD[0], bass.IndirectOffsetOnAxis(ap=dI[:, j, g:g + 1], axis=0)),
                                yg_free[s], t_prev, sig=S(f"d_yg{s}", 16))
                        a = DV.go(lambda e, s=s, k=k, t=t, g=g: e.scalar_tensor_tensor(
                            X[:, k, t], yg[:, s, 0], w1[:, g:g + 1], X[:, k, t], ALU.mult, ALU.add), tx, ty, sig=S("v_cb"))
                        yg_free[s] = DV.go(lambda e, s=s, k=k, t=t, g=g: e.scalar_tensor_tensor(
                            X[:, k, t], yg[:, s, 1], w2[:, g:g + 1], X[:, k, t], ALU.mult, ALU.add), a, sig=S("v_cb"))
                    t_x[bt] = yg_free[(cnt["yg"] - 1) % 2]

                def norm(src, dst, ready, free):
                    ts = None
                    for t in range(TT):
                        ts = DV.go(lambda e, t=t: e.bn_stats(st[:, t], src(t)), ready, sig=S("v_st"))
                    for t in range(TT):
                        ta = DV.go(lambda e, t=t: e.bn_aggr(mv[:, t], st[:, t]), ts, sig=S("v_ag"))
                    tp = PO.go(lambda e: e.tensor_scalar(ve[:], mv[:, :, 1], 1e-5, None, ALU.add), ta, sig=S("p_ve"))
                    tp = PO.go(lambda e: e.tensor_tensor(rstd[:], ve[:], mhalf[:], ALU.pow), tp, sig=S("p_rs"))
                    for t in range(TT):
                        tn = DV.go(lambda e, t=t: e.tensor_scalar(dst[:, t], src(t), mv[:, t, 0:1], rstd[:, t:t + 1],
                                                                  ALU.subtract, ALU.mult), tp, free, sig=S("v_xn"))
                    return tn

                t_xn, xn_used = {}, [None]

                def pre(bt):
                    k = bt % 2
                    t_xn[bt] = norm(lambda t: X[:, k, t], xn, t_x[bt], xn_used[0])
                    if A:
                        for t in range(TT):
                            t_xpre[bt] = PO.go(lambda e, t=t: e.tensor_tensor(X[:, k, t], X[:, k, t], bout[:], ALU.add),
                                               t_xn[bt], sig=S("p_xb"))
                    else:
                        t_xpre[bt] = t_xn[bt]

                def transpose4(src, kc, ready):
                    for t in range(TT):
                        tp = PE.go(lambda e, t=t: e.transpose(bank[B_M][:, t * 128:(t + 1) * 128],
                                                             src[:, t, kc * 128:(kc + 1) * 128], ident),
                                   ready, bank_free[B_M], sig=S("m_tr") if t == TT - 1 else None)
                    return tp

                def xpose(bt, kc):
                    tp = transpose4(xn, kc, t_xn[bt])
                    if kc == 1:
                        xn_used[0] = tp
                    a = AC.go(lambda e: e.copy(xTh[:, kc], bank[B_M][:]), tp, xT_used[0], sig=S("a_xT"))
                    v = DV.go(lambda e: e.tensor_tensor(xTl[:, kc], bank[B_M][:], xTh[:, kc].bitcast(F32),
                                                        ALU.subtract), a, xT_used[0], sig=S("v_xT"))
                    bank_free[B_M] = [v]
                    t_xT[bt] = [a, v]

                def mm3(out, lh, ll, rh, rl, first, last, sig, *tok):
                    PE.go(lambda e: e.matmul(out, lh, rh, start=first, stop=False), *tok)
                    PE.go(lambda e: e.matmul(out, lh, rl, start=False, stop=False))
                    return PE.go(lambda e: e.matmul(out, ll, rh, start=False, stop=last), sig=sig if last else None)

                def proj(u):
                    bt, p = divmod(u, 8)
                    k = u % 2
                    toks = []
                    for j, (H, L) in enumerate(((Qh, Ql), (Kh, Kl))):
                        bk = bank[B_Q[j]]
                        c0 = j * 1024 + p * 128
                        for kc in range(2):
                            tp = mm3(bk[:], Wh[:, kc, c0:c0 + 128], Wl[:, kc, c0:c0 + 128], xTh[:, kc], xTl[:, kc],
                                     kc == 0, kc == 1, S("m_qk"), t_w, t_xT[bt], bank_free[B_Q[j]])
                        used = qk_used.get(u - 2)
                        if A:
                            sc = 0.125 if j == 0 else 1.0
                            a = AC.go(lambda e, H=H, bk=bk, sc=sc: e.activation(H[:, k], bk[:], ACT.Copy, scale=sc),
                                      tp, used, sig=S("a_qk"))
                            v = DV.go(lambda e, H=H, L=L, bk=bk, sc=sc: e.scalar_tensor_tensor(
                                L[:, k], bk[:], sc, H[:, k].bitcast(F32), ALU.mult, ALU.subtract),
                                a, used, sig=S("v_qk"))
                            bank_free[B_Q[j]] = [v]
                            toks += [a, v]
                        else:
                            rj = rp[:, j]
                            pf = rope_free[j]
                            DV.go(lambda e, bk=bk, rj=rj: e.tensor_tensor(rj[:, 0], bk[:], tab[:, 1], ALU.mult),
                                  tp, pf, sig=S("v_rp"))
                            DV.go(lambda e, bk=bk, rj=rj: e.tensor_tensor(
                                rj[0:64, 1], bk[64:128, :], tab[64:128, 2], ALU.mult), sig=S("v_rp"))
                            v = DV.go(lambda e, bk=bk, rj=rj: e.tensor_tensor(
                                rj[64:128, 1], bk[0:64, :], tab[0:64, 2], ALU.mult), sig=S("v_rp"))
                            bank_free[B_Q[j]] = [v]
                            g = PO.go(lambda e, j=j, rj=rj: e.tensor_tensor(rf[:, j], rj[:, 0], rj[:, 1], ALU.add),
                                      v, rf_free[j], sig=S("p_rf"))
                            rope_free[j] = g
                            a = AC.go(lambda e, H=H, j=j: e.copy(H[:, k], rf[:, j]), g, used, sig=S("a_qk"))
                            l = PO.go(lambda e, H=H, L=L, j=j: e.tensor_tensor(
                                L[:, k], rf[:, j], H[:, k].bitcast(F32), ALU.subtract), a, used, sig=S("p_lo"))
                            rf_free[j] = [a, l]
                            toks += [a, l]
                    t_q[u] = toks
                    if p % 4 == 0:
                        g = u // 4
                        vk = g % 2
                        c0 = 2048 + (p // 4) * 512
                        vt = []
                        for t in range(TT):
                            j = t % 2
                            bk = bank[B_Q[j]]
                            ts = slice(t * 128, (t + 1) * 128)
                            for kc in range(2):
                                tp = mm3(bk[:], xTh[:, kc, ts], xTl[:, kc, ts], Wh[:, kc, c0:c0 + 512],
                                         Wl[:, kc, c0:c0 + 512], kc == 0, kc == 1, S("m_v"), bank_free[B_Q[j]])
                            if j == 0:
                                a = AC.go(lambda e, t=t, bk=bk: e.copy(V[:, vk, t], bk[:]), tp, v_used.get(g - 2), sig=S("a_v"))
                            else:
                                a = DV.go(lambda e, t=t, bk=bk: e.tensor_copy(V[:, vk, t], bk[:]), tp, v_used.get(g - 2),
                                          sig=S("v_v"))
                            bank_free[B_Q[j]] = [a]
                            vt.append(a)
                        t_v[g] = vt
                    if p % 4 == 0:
                        xT_used[0] = tp
                    else:
                        xT_used[0] = tp

                rope_free, rf_free = [None, None], [None, None]

                def scores(h):
                    u, hl = divmod(h, HU)
                    k = u % 2
                    r = slice(64 * hl, 64 * hl + 64) if A else slice(0, 128)
                    pb = h % NP
                    tb = tab[:, h % 16] if A else tab[:, 0]
                    for t in range(TT):
                        s = B_S[cnt["s"] % 2]
                        cnt["s"] += 1
                        w = (t + 1) * 128
                        ts = slice(t * 128, w)
                        tp = mm3(bank[s][:, 0:w], Qh[r, k, ts], Ql[r, k, ts], Kh[r, k, 0:w], Kl[r, k, 0:w],
                                 True, True, S("m_s"), t_q[u], bank_free[s])
                        v = DV.go(lambda e, s=s, w=w, t=t: e.tensor_tensor_reduce(
                            out=P[:, pb, OFF[t]:OFF[t] + w], in0=bank[s][:, 0:w], in1=tb[:, 512 - w:512], scale=1.0,
                            scalar=-3e38, op0=ALU.add, op1=ALU.max, accum_out=mx[:, pb, t:t + 1]),
                            tp, t_tab, p_used.get(h - NP), sig=S("v_mx"))
                        bank_free[s] = [v]
                    qk_used[u] = tp
                    sc = 1.0 if A else 1.0 / 128
                    n = DV.go(lambda e: e.tensor_scalar(nm[:, pb], mx[:, pb], -sc, None, ALU.mult), v, sig=S("v_nm"))
                    for t in range(TT):
                        ps = P[:, pb, OFF[t]:OFF[t] + (t + 1) * 128]
                        a = AC.go(lambda e, ps=ps, t=t: e.activation(ps, ps, ACT.Exp, bias=nm[:, pb, t:t + 1], scale=sc,
                                                                     accum_out=rs[:, pb, t:t + 1]), n, sig=S("a_exp"))
                    p_exp[h] = a

                def scale(h):
                    pb = h % NP
                    r = DV.go(lambda e: e.reciprocal(rc[:, pb], rs[:, pb]), p_exp[h], sig=S("v_rc"))
                    for t in range(TT):
                        ps = P[:, pb, OFF[t]:OFF[t] + (t + 1) * 128]
                        v = DV.go(lambda e, ps=ps, t=t: e.tensor_scalar(ps, ps, rc[:, pb, t:t + 1], None, ALU.mult),
                                  r, sig=S("v_sc"))
                    p_ready[h] = v

                def flip(h):
                    pb = h % NP
                    pt = h % 2
                    toks = []
                    for cs in ((0,), (1, 3), (2,)):
                        s = B_T[cnt["t"] % 2]
                        cnt["t"] += 1
                        at = 0
                        for cc in cs:
                            for t in range(cc, TT):
                                lastone = cc == cs[-1] and t == TT - 1
                                tp = PE.go(lambda e, at=at, s=s, t=t, cc=cc: e.transpose(
                                    bank[s][:, at:at + 128], P[:, pb, OFF[t] + cc * 128:OFF[t] + cc * 128 + 128], ident),
                                    p_ready[h], bank_free[s], sig=S("m_t") if lastone else None)
                                at += 128
                        dst = PT[:, pt, PTO[cs[0]]:PTO[cs[0]] + at]
                        if cs == (1, 3):
                            x = DV.go(lambda e, dst=dst, s=s, at=at: e.tensor_copy(dst, bank[s][:, 0:at]), tp,
                                      pt_used.get(h - 2), sig=S("v_pt"))
                        else:
                            x = AC.go(lambda e, dst=dst, s=s, at=at: e.copy(dst, bank[s][:, 0:at]), tp,
                                      pt_used.get(h - 2), sig=S("a_pt"))
                        bank_free[s] = [x]
                        toks.append(x)
                    p_used[h] = tp
                    pt_ready[h] = toks

                def attend(u):
                    bt, p = divmod(u, 8)
                    g = u // 4
                    vk = g % 2
                    o = bank[B_O]
                    for cc in range(TT):
                        for hl in range(HU):
                            h = u * HU + hl
                            col = (u % 4) * 128 + hl * 64
                            w = 512 - cc * 128
                            out = o[64 * hl:64 * hl + 64, cc * 128:512] if A else o[:, cc * 128:512]
                            lastone = cc == TT - 1 and hl == HU - 1
                            tp = PE.go(lambda e, out=out, cc=cc, col=col, h=h, w=w: e.matmul(
                                out, V[:, vk, cc, col:col + KD], PT[:, h % 2, PTO[cc]:PTO[cc] + w],
                                start=cc == 0, stop=cc == TT - 1), pt_ready[h], t_v[g], bank_free[B_O],
                                sig=S("m_o") if lastone else None)
                    for hl in range(HU):
                        pt_used[u * HU + hl] = tp
                    if u % 4 == 3:
                        v_used[g] = tp
                    a = AC.go(lambda e: e.copy(OT[:, p], o[:]), tp, ot_used.get(bt - 1), sig=S("a_o"))
                    bank_free[B_O] = [a]
                    if p == 7:
                        t_ot[bt] = a

                t_ot = {}
                t_x1 = {}

                def outproj(bt, half):
                    k = bt % 2
                    for t2 in range(2):
                        t = half * 2 + t2
                        for ch in range(8):
                            tp = PE.go(lambda e, t=t, t2=t2, ch=ch: e.matmul(
                                bank[B_M][:, t2 * 256:t2 * 256 + 256], OT[:, ch, t * 128:(t + 1) * 128], WO[:, ch],
                                start=ch == 0, stop=ch == 7), t_ot[bt], t_w, bank_free[B_M],
                                sig=S("m_y") if t2 == 1 and ch == 7 else None)
                    if half == 1:
                        ot_used[bt] = tp
                    v = DV.go(lambda e: e.tensor_tensor(X[:, k, 2 * half:2 * half + 2], bank[B_M][:].rearrange(
                        "p (t d) -> p t d", t=2), X[:, k, 2 * half:2 * half + 2], ALU.add), tp, t_xpre[bt], sig=S("v_x1"))
                    bank_free[B_M] = [v]
                    t_x1[bt] = v

                hold = {"hh": None, "xs": None, "xl": None, "hT": None, "lg": None}
                t_hh = {}

                def gate_norm(bt):
                    k = bt % 2
                    xl = xn
                    tn = norm(lambda t: X[:, k, t], xl, t_x1[bt], xn_used[0])
                    for t in range(TT):
                        ta = AC.go(lambda e, t=t: e.activation(xs[:, t], xl[:, t], ACT.Square,
                                                               accum_out=ss[:, t:t + 1]), tn, hold["xs"], sig=S("a_ss"))
                    tg = PO.go(lambda e: e.tensor_scalar(ve[:], ss[:], 1.0 / D, float(np.finfo(np.float32).eps),
                                                         ALU.mult, ALU.add), ta, sig=S("p_v2"))
                    tg = PO.go(lambda e: e.tensor_tensor(r2[:], ve[:], mhalf[:], ALU.pow), tg, sig=S("p_r2"))
                    for t in range(TT):
                        th = DV.go(lambda e, t=t: e.scalar_tensor_tensor(hh[:, t], xl[:, t], r2[:, t:t + 1], nw[:],
                                                                         ALU.mult, ALU.mult), tg, hold["hh"], sig=S("v_h"))
                    tx = PO.go(lambda e: e.tensor_tensor(xs[:], X[:, k], xl[:], ALU.add), ta, tn, sig=S("p_xs"))
                    xn_used[0] = [th, tx]
                    t_y[bt] = [tx]
                    dh = dma(hD[ph].rearrange("(b t p) d -> b p t d", p=128, t=TT)[bt], hh[:], "d_h", th)
                    dx = dma(rD[ph].rearrange("(b t p) d -> b p t d", p=128, t=TT)[bt], xs[:], "d_r", tx)
                    hold["xs"] = [dx]
                    hold["hh"] = [dh]
                    t_hh[bt] = th

                t_hT = {}

                def gate_flip(bt, kc):
                    tp = transpose4(hh, kc, t_hh[bt])
                    a = AC.go(lambda e: e.copy(hT[:, kc], bank[B_M][:]), tp, hold["hT"], sig=S("a_hT"))
                    bank_free[B_M] = [a]
                    t_hT[bt] = a
                    if kc == 1:
                        hold["hh"] = hold["hh"] + [tp]

                def gate_top(bt):
                    for t in range(TT):
                        for kc in range(2):
                            tp = PE.go(lambda e, t=t, kc=kc: e.matmul(
                                bank[B_M][:, t * E:(t + 1) * E], hT[:, kc, t * 128:(t + 1) * 128], gw[:, kc],
                                start=kc == 0, stop=kc == 1), t_hT[bt], bank_free[B_M],
                                sig=S("m_lg") if t == TT - 1 and kc == 1 else None)
                    hold["hT"] = tp
                    v = DV.go(lambda e: e.tensor_tensor(lg[:], bank[B_M][:, 0:TT * E].rearrange("p (t k) -> p t k", k=E),
                                                        gb[:].rearrange("p (a k) -> p a k", a=1).broadcast_to(
                                                            [128, TT, E]), ALU.add), tp, hold["lg"], sig=S("v_lg"))
                    bank_free[B_M] = [v]
                    for t in range(TT):
                        v1 = DV.go(lambda e, t=t: e.max(v8[:, t], lg[:, t]), v, sig=S("v_m8"))
                    for t in range(TT):
                        v2 = DV.go(lambda e, t=t: e.max_index(i8[:, t], v8[:, t], lg[:, t]), v1, sig=S("v_i8"))
                    v2 = DV.go(lambda e: e.tensor_copy(if8[:], i8[:]), v2, sig=S("v_if"))
                    v3 = DV.go(lambda e: e.tensor_tensor(dv[:], v8[:, :, 1], v8[:, :, 0], ALU.subtract), v1, sig=S("v_dv"))
                    g0 = bt * TT
                    io = cst[:, C_I8:C_I8 + E].rearrange("p (a k) -> p a k", a=1).broadcast_to([128, TT, E])
                    for j, M in enumerate((M1, M2)):
                        m = DV.go(lambda e, j=j, M=M: e.tensor_tensor(
                            M[:, g0:g0 + TT], io, if8[:, :, j:j + 1].broadcast_to([128, TT, E]), ALU.is_equal),
                            v2, sig=S("v_M"))
                    a = AC.go(lambda e: e.activation(dv[:], dv[:], ACT.Exp), v3, sig=S("a_ev"))
                    v4 = DV.go(lambda e: e.tensor_scalar(w1[:, g0:g0 + TT], dv[:], 1.0, None, ALU.add), a, sig=S("v_w"))
                    v5 = DV.go(lambda e: e.reciprocal(w1[:, g0:g0 + TT], w1[:, g0:g0 + TT]), v4, sig=S("v_w"))
                    v6 = DV.go(lambda e: e.tensor_tensor(w2[:, g0:g0 + TT], w1[:, g0:g0 + TT], dv[:], ALU.mult), v5,
                               sig=S("v_w"))
                    hold["lg"] = v6
                    return m

                load_x(0)
                pre(0)
                xpose(0, 0)
                xpose(0, 1)
                proj(0)
                for h in range(HU):
                    scores(h)
                proj(1)
                for h in range(HU):
                    scale(h)
                for u in range(NU):
                    bt, p = divmod(u, 8)
                    if p == 3 and bt + 1 < NB:
                        load_x(bt + 1)
                    for hl in range(HU):
                        h = u * HU + hl
                        n = h + HU
                        if n < NU * HU:
                            scores(n)
                        flip(h)
                        if A and n - 1 >= HU and n - 1 < NU * HU:
                            scale(n - 1)
                    if A and n == NU * HU:
                        pass
                    if bt >= 1:
                        if p == 0:
                            outproj(bt - 1, 0)
                        elif p == 2:
                            gate_flip(bt - 1, 0)
                        elif p == 3:
                            gate_top(bt - 1)
                    if u + 2 < NU:
                        proj(u + 2)
                    if bt >= 1:
                        if p == 0:
                            outproj(bt - 1, 1)
                            gate_norm(bt - 1)
                        elif p == 2:
                            gate_flip(bt - 1, 1)
                    if p == 4 and bt + 1 < NB:
                        pre(bt + 1)
                    if p == 5 and bt + 1 < NB:
                        xpose(bt + 1, 0)
                    attend(u)
                    if p == 5 and bt + 1 < NB:
                        xpose(bt + 1, 1)
                    if not A and h + 1 < NU * HU:
                        scale(h + 1)
                bt = NB - 1
                outproj(bt, 0)
                outproj(bt, 1)
                gate_norm(bt)
                gate_flip(bt, 0)
                gate_flip(bt, 1)
                t_M = gate_top(bt)
            ends = [S(n) for n in sems if n[0] in "mavpd"]
            return [(s, s.n) for s in ends if s.n], t_M

        def experts(ph, t_end, t_M, last):
            c = ExitStack()

            def b(name, shape, dt=F32):
                return sb(f"{name}f_{ph}", shape, dt, c)

            with c:
                W1h = b("W1h", [128, E, 2, 512], F32R)
                W1l = b("W1l", [128, E, 2, 512], F32R)
                W2 = b("W2", [128, E, 2, D])
                bl = b("bl", [1, 2, 512], F32R)
                bl_free, t_br = [None, None], [None, None]
                BR = b("BR", [2, E * 768], F32R)
                on2 = b("on2", [2, 128], F32R)
                Ms = b("Ms", [128, NT, E])
                Tt = b("Tt", [128, NT, E])
                inc = b("inc", [128, NT, E])
                tmp = b("tmp", [128, NT, E])
                tm2 = b("tm2", [128, NT, E])
                one = b("one", [128, NT])
                n8 = b("n8", [128, 4, E])
                ni = b("ni", [128, E], I32)
                dF = b("dF", [128, 2, NT])
                ia = b("ia", [128, 2, NT], I32)
                fa = b("fa", [128, 2, NT])
                fb = b("fb", [128, 2, NT])
                ob = b("ob", [128, 4, 128], F32R)
                oa = b("oa", [128, 4, NSP], F32R)
                se = b("se", [1, NSP, E])
                ef = b("ef", [1, NSP])
                G = b("G", [128, 4, D])
                XTh = b("XTh", [128, 2, 2, 128], F32R)
                XTl = b("XTl", [128, 2, 2, 128], F32R)
                gl = b("gl", [128, 2, HID])
                li = b("li", [128, 2, HID])
                sg = b("sg", [128, 2, HID])
                ac = b("ac", [128, 2, HID])
                AT = b("AT", [128, 2, 2, 128])
                Y = b("Y", [128, 2, D])
                for q in (PE, AC, DV, PO, SP):
                    q.wait(t_end)

                v = DV.go(lambda e: e.tensor_tensor(Ms[:], M1[:], M2[:], ALU.add), t_M, sig=S("r_v"))
                flat = Ms[:].rearrange("p t k -> p (t k)")
                ones = b("ones", [128, 128])
                vo = DV.go(lambda e: e.memset(ones[:], 1.0), sig=S("r_v"))
                von = DV.go(lambda e: e.memset(one[:], 1.0), sig=S("r_v"))
                PE.go(lambda e: e.matmul(bank[0][:, 0:256], cst[:, C_TRI:C_TRI + 128], flat, start=True, stop=True), v, vo)
                t_rk = PE.go(lambda e: e.matmul(bank[1][:, 0:256], ones[:], flat, start=True, stop=True), sig=S("r_m"))
                v = DV.go(lambda e: e.tensor_copy(Tt[:].rearrange("p t k -> p (t k)"), bank[1][:, 0:256]), t_rk, sig=S("r_v"))
                for k in range(E):
                    vs = DV.go(lambda e, k=k: e.tensor_tensor_scan(inc[:, :, k], one[:], Tt[:, :, k], 0.0,
                                                                  ALU.mult, ALU.add), v, von, sig=S("r_v"))
                v1 = DV.go(lambda e: e.tensor_scalar(n8[:, 0], inc[:, NT - 1], 127.0, None, ALU.add), vs, sig=S("r_v"))
                v1 = DV.go(lambda e: e.tensor_copy(ni[:], n8[:, 0]), v1, sig=S("r_v"))
                v1 = DV.go(lambda e: e.tensor_single_scalar(ni[:], ni[:], 7, ALU.arith_shift_right), v1, sig=S("r_v"))
                v1 = DV.go(lambda e: e.tensor_copy(n8[:, 1], ni[:]), v1, sig=S("r_v"))
                v1 = DV.go(lambda e: e.tensor_tensor_scan(n8[:, 2], one[:, 0:E], n8[:, 1], 0.0, ALU.mult, ALU.add), v1,
                           sig=S("r_v"))
                t_inc = v1
                v1 = DV.go(lambda e: e.tensor_tensor(n8[:, 3], n8[:, 2], n8[:, 1], ALU.subtract), v1, sig=S("r_v"))
                v1 = DV.go(lambda e: e.tensor_scalar(n8[:, 3], n8[:, 3], 128.0, None, ALU.mult), v1, sig=S("r_v"))
                v2 = DV.go(lambda e: e.tensor_tensor(tmp[:], inc[:], Tt[:], ALU.subtract), vs, sig=S("r_v"))
                v2 = DV.go(lambda e: e.tensor_tensor(tmp[:].rearrange("p t k -> p (t k)"), bank[0][:, 0:256],
                                                     tmp[:].rearrange("p t k -> p (t k)"), ALU.add), v2, sig=S("r_v"))
                v2 = DV.go(lambda e: e.tensor_tensor(tmp[:], tmp[:], n8[:, 3:4].broadcast_to([128, NT, E]), ALU.add),
                           v2, v1, sig=S("r_v"))
                for j, M in enumerate((M1, M2)):
                    v3 = DV.go(lambda e, M=M: e.tensor_tensor(tm2[:], M[:], tmp[:], ALU.mult), v2, sig=S("r_v"))
                    v2 = DV.go(lambda e, j=j: e.reduce_sum(dF[:, j], tm2[:], AX), v3, sig=S("r_v"))
                v2 = DV.go(lambda e: e.tensor_copy(dI[:], dF[:]), v2, sig=S("r_v"))
                t_dI = v2
                v2 = DV.go(lambda e: e.tensor_single_scalar(ia[:], dI[:], 7, ALU.arith_shift_right), v2, sig=S("r_v"))
                v2 = DV.go(lambda e: e.tensor_copy(fa[:], ia[:]), v2, sig=S("r_v"))
                v2 = DV.go(lambda e: e.scalar_tensor_tensor(fb[:], fa[:], -128.0, dF[:], ALU.mult, ALU.add), v2, sig=S("r_v"))
                v4 = DV.go(lambda e: e.tensor_tensor(
                    se[:], cst[0:1, C_IOTA:C_IOTA + NSP].rearrange("p (s a) -> p s a", a=1).broadcast_to([1, NSP, E]),
                    n8[0:1, 2:3, :].broadcast_to([1, NSP, E]), ALU.is_ge), t_inc, sig=S("r_v"))
                v4 = DV.go(lambda e: e.reduce_sum(ef[:], se[:], AX), v4, sig=S("r_v"))
                v4 = DV.go(lambda e: e.tensor_scalar(ef[:], ef[:], float(E - 1), None, ALU.min), v4, sig=S("r_v"))
                t_et = DV.go(lambda e: e.tensor_copy(etab[:], ef[:]), v4, sig=S("r_v"))
                ob_free = [None] * 4
                for g in range(2 * NT):
                    t, j = divmod(g, 2)
                    k = g % 4
                    x = DV.go(lambda e, k=k, t=t, j=j: e.tensor_scalar(ob[:, k], cst[:, C_IOTA:C_IOTA + 128],
                                                                       fb[:, j, t:t + 1], None, ALU.is_equal),
                              v2, ob_free[k], sig=S("r_ob"))
                    y = DV.go(lambda e, k=k, t=t, j=j: e.tensor_scalar(
                        oa[:, k], cst[:, C_IOTA:C_IOTA + NSP], fa[:, j, t:t + 1], cst[:, C_TOK + t:C_TOK + t + 1],
                        ALU.is_equal, ALU.mult), v2, ob_free[k], sig=S("r_oa"))
                    ob_free[k] = PE.go(lambda e, k=k, g=g: e.matmul(bank[2][:, 0:NSP], ob[:, k], oa[:, k],
                                                                    start=g == 0, stop=g == 2 * NT - 1), x, y, sig=S("r_id"))
                t_idx = DV.go(lambda e: e.tensor_copy(idx[:], bank[2][:, 0:NSP]), ob_free[k], sig=S("r_v"))

                for i in range(E * 768 // 512):
                    k, cs = i % 2, slice(i * 512, (i + 1) * 512)
                    tb = dma(stage[0:1, k, :], T["mlp_b"][:, cs], f"d_stage{k}", st_free[k])
                    a1 = AC.go(lambda e, k=k, cs=cs: e.copy(BR[0:1, cs], stage[0:1, k, :]), tb, sig=S("a_bh"))
                    a2 = DV.go(lambda e, k=k, cs=cs: e.tensor_tensor(
                        bl[0:1, k, :], stage[0:1, k, :], BR[0:1, cs].bitcast(F32), ALU.subtract), a1, bl_free[k],
                        sig=S("v_bl"))
                    st_free[k] = [a1, a2]
                    tbr = bl_free[k] = dma(BR[1:2, cs].bitcast(F32), bl[0:1, k, :].bitcast(F32), f"d_bl{k}", a2)
                    t_br[k] = [tbr, a1]
                von2 = DV.go(lambda e: e.tensor_copy(on2[:], ones[0:2, :]), vo, sig=S("r_v"))
                tbr = t_br
                tw = split_load([(T["w1"][:, k], W1h[:, k].rearrange("p a b -> p (a b)"),
                                  W1l[:, k].rearrange("p a b -> p (a b)")) for k in range(E)])
                tw2 = dma(W2[:], T["w2"], "d_w2")

                g_free, t_g = {}, {}
                xt_free, t_xt = {}, {}
                gl_free, t_ac = {}, {}
                at_free, y_free = {}, {}
                bf = {i: [t_idx] for i in range(8)}
                B1, BX, BA, BY = (0, 1), (2, 3), (4, 5), (6, 7)
                y_out = yD[ph].rearrange("(s p) d -> s p d", p=128)
                t_yd = []

                def gather(a):
                    t_g[a] = PO.go(lambda e: e.indirect_dma_start(G[:, a % 4], None, hD[ph], bass.IndirectOffsetOnAxis(
                        ap=idx[:, a:a + 1], axis=0)), t_idx, g_free.get(a - 4), sig=S(f"d_g{a % 4}", 16))

                def flip_x(a):
                    k = a % 2
                    bk = bank[BX[k]]
                    for kc in range(2):
                        tp = PE.go(lambda e, kc=kc: e.transpose(bk[:, kc * 128:(kc + 1) * 128],
                                                               G[:, a % 4, kc * 128:(kc + 1) * 128], ident),
                                   t_g[a], bf[BX[k]], sig=S("f_x") if kc else None)
                    g_free[a] = tp
                    src = bk[:, 0:256].rearrange("p (a b) -> p a b", a=2)
                    x = AC.go(lambda e: e.copy(XTh[:, k], src), tp, xt_free.get(a - 2), sig=S("a_fx"))
                    y = DV.go(lambda e: e.tensor_tensor(XTl[:, k], src, XTh[:, k].bitcast(F32), ALU.subtract), x,
                              xt_free.get(a - 2), sig=S("v_fx"))
                    bf[BX[k]] = [y]
                    t_xt[a] = [x, y]

                def up(a):
                    k = a % 2
                    bk = bank[B1[k]]
                    PE.wait(t_et, tw, tbr, von2, t_xt[a], bf[B1[k]])

                    def f(e):
                        r = e.value_load(etab[0:1, a:a + 1], min_val=0, max_val=E - 1)
                        ex = bass.ds(r, 1)
                        bias = BR[:, 0:E * 512].rearrange("q (x n) -> q x n", x=E)
                        e.matmul(bk[:], on2[:], bias[:, ex].rearrange("q x n -> q (x n)"), start=True, stop=False)
                        for kc in range(2):
                            wh = W1h[:, ex, kc].rearrange("p x n -> p (x n)")
                            wl = W1l[:, ex, kc].rearrange("p x n -> p (x n)")
                            e.matmul(bk[:], XTh[:, k, kc], wh, start=False, stop=False)
                            e.matmul(bk[:], XTh[:, k, kc], wl, start=False, stop=False)
                            i = e.matmul(bk[:], XTl[:, k, kc], wh, start=False, stop=kc == 1)
                        return i
                    tp = PE.go(f, sig=S("f_up"))
                    xt_free[a] = tp
                    g = DV.go(lambda e: e.tensor_scalar(gl[:, k], bk[:, 0:HID], LIMIT, None, ALU.min), tp, gl_free.get(a - 2),
                              sig=S("v_gl"))
                    s = AC.go(lambda e: e.activation(sg[:, k], gl[:, k], ACT.Sigmoid, scale=ALPHA), g, gl_free.get(a - 2),
                              sig=S("a_sg"))
                    l = DV.go(lambda e: e.tensor_scalar(li[:, k], bk[:, HID:2 * HID], LIMIT, -LIMIT, ALU.min, ALU.max), tp,
                              gl_free.get(a - 2), sig=S("v_li"))
                    bf[B1[k]] = [l]
                    m = DV.go(lambda e: e.scalar_tensor_tensor(li[:, k], li[:, k], 1.0, gl[:, k], ALU.add, ALU.mult), l, g,
                              sig=S("v_lg2"))
                    m = DV.go(lambda e: e.tensor_tensor(ac[:, k], li[:, k], sg[:, k], ALU.mult), m, s, at_free.get(a - 2),
                              sig=S("v_ac"))
                    gl_free[a] = m
                    t_ac[a] = m

                t_at = {}

                def flip_a(a):
                    k = a % 2
                    bk = bank[BA[k]]
                    for kc in range(2):
                        tp = PE.go(lambda e, kc=kc: e.transpose(bk[:, kc * 128:(kc + 1) * 128],
                                                               ac[:, k, kc * 128:(kc + 1) * 128], ident),
                                   t_ac[a], bf[BA[k]], sig=S("f_a") if kc else None)
                    at_free[a] = tp
                    src = bk[:, 0:256].rearrange("p (a b) -> p a b", a=2)
                    x = AC.go(lambda e: e.copy(AT[:, k], src), tp, t_dn.get(a - 2), sig=S("a_at"))
                    bf[BA[k]] = [x]
                    t_at[a] = x

                t_dn = {}

                def down(a):
                    k = a % 2
                    bk = bank[BY[k]]
                    PE.wait(tw2, t_at[a], bf[BY[k]])

                    def f(e):
                        r = e.value_load(etab[0:1, a:a + 1], min_val=0, max_val=E - 1)
                        ex = bass.ds(r, 1)
                        bias = BR[:, E * 512:E * 768].rearrange("q (x n) -> q x n", x=E)
                        e.matmul(bk[:, 0:D], on2[:], bias[:, ex].rearrange("q x n -> q (x n)"), start=True, stop=False)
                        for kc in range(2):
                            i = e.matmul(bk[:, 0:D], AT[:, k, kc], W2[:, ex, kc].rearrange("p x n -> p (x n)"),
                                         start=False, stop=kc == 1)
                        return i
                    tp = PE.go(f, sig=S("f_dn"))
                    t_dn[a] = tp
                    x = AC.go(lambda e: e.copy(Y[:, k], bk[:, 0:D]), tp, y_free.get(a - 2), sig=S("a_y"))
                    bf[BY[k]] = [x]
                    y_free[a] = dma(y_out[a], Y[:, k], f"d_y{k}", x)

                for a in range(3):
                    gather(a)
                flip_x(0)
                up(0)
                flip_x(1)
                for a in range(NS):
                    if a + 3 < NS:
                        gather(a + 3)
                    flip_a(a)
                    if a + 2 < NS:
                        flip_x(a + 2)
                    if a + 1 < NS:
                        up(a + 1)
                    down(a)
                t_yd = [y_free[NS - 1], y_free[NS - 2]]

                if last:
                    yg = WO[:].rearrange("p (s j) d -> p s j d", j=2)
                    xr = G
                    o_free = [t_yd] * 4
                    prev = rD[1].rearrange("(t p) d -> t p d", p=128)
                    outv = T["out"].rearrange("b (t p) d -> (b t) p d", p=128)
                    for g in range(NT):
                        s = g % 4
                        tx = dma(xr[:, s], prev[g], f"d_xr{s}", o_free[s])
                        for j in range(2):
                            ty = PO.go(lambda e, s=s, j=j, g=g: e.indirect_dma_start(
                                yg[:, s, j, :], None, yD[1], bass.IndirectOffsetOnAxis(ap=dI[:, j, g:g + 1], axis=0)),
                                o_free[s], t_yd, t_dI, sig=S(f"d_yl{s}", 16))
                        x = DV.go(lambda e, s=s, g=g: e.scalar_tensor_tensor(
                            xr[:, s], yg[:, s, 0], w1[:, g:g + 1], xr[:, s], ALU.mult, ALU.add), tx, ty, sig=S("v_fin"))
                        x = DV.go(lambda e, s=s, g=g: e.scalar_tensor_tensor(
                            xr[:, s], yg[:, s, 1], w2[:, g:g + 1], xr[:, s], ALU.mult, ALU.add), x, sig=S("v_fin"))
                        o_free[s] = AC.go(lambda e, s=s, g=g: e.dma_start(outv[g], xr[:, s]), x, sig=S(f"d_out{s}", 16))
                    SP.wait(o_free)
                    AC.wait(o_free)
            ends = [(s, s.n) for n, s in sems.items() if s.n]
            return ends, t_yd

        t_w = load_attention(0)
        t_end, t_M = attention(0, t_w, None, None)
        t_end, t_yd = experts(0, t_end, t_M, False)
        t_w = load_attention(1, t_end)
        t_end, t_M = attention(1, t_w, t_end, t_yd)
        t_end, t_yd = experts(1, t_end, t_M, True)

        block = ctx.enter_context(nc.Block())

        @block.sync
        def _(e):
            SP.play(e)

        @block.scalar
        def _(e):
            AC.play(e)

        @block.vector
        def _(e):
            DV.play(e)

        @block.gpsimd
        def _(e):
            PO.play(e)

        @block.tensor
        def _(e):
            PE.play(e)


def constants():
    f = np.float32
    cst = np.zeros((128, C_N), f)
    p = np.arange(128)
    cst[:, C_ID:C_ID + 128] = np.eye(128)
    cst[:, C_IOTA:C_IOTA + 128] = p[None, :]
    cst[:, C_TRI:C_TRI + 128] = p[:, None] < p[None, :]
    cst[:, C_P] = p
    cst[:, C_TOK:C_TOK + NT] = np.arange(NT)[None, :] * 128 + p[:, None]
    cst[:, C_I8:C_I8 + 8] = np.arange(8)[None, :]
    start = 2 ** (-2 ** (-(log2(16) - 3)))
    slopes = np.array([start * start ** i for i in range(16)], f)
    c = np.arange(512)
    rel = -np.abs((c[None, :] - 384) - p[:, None]).astype(f)
    seen = (c[None, :] - 384) <= p[:, None]
    alibi = np.where(seen[None], rel[None] * slopes[:, None, None], f(-1e30)).astype(f)
    half = 64
    dims = np.arange(half, dtype=f)
    freq = np.power(f(10000.0), -dims / f(half)).astype(f)
    rad = np.arange(N, dtype=f)[:, None] * freq[None, :]
    cos, sin = np.cos(rad).astype(f).T, np.sin(rad).astype(f).T
    rope = np.zeros((128, 3, 512), f)
    rope[:, 0] = np.where(seen, f(0), f(-1e32))
    rope[:, 1] = np.concatenate([cos, cos])
    rope[:, 2] = np.concatenate([sin, -sin])
    return {"c_cst": cst, "c_alibi": np.ascontiguousarray(alibi.transpose(1, 0, 2)), "c_rope": rope}


def kernel(**inputs):
    import numpy as _np
    import concourse.bacc as _bacc
    from concourse import mybir as _mybir
    from concourse.bass_utils import run_bass_kernel_spmd as _run

    g = {k[3:]: _np.asarray(v) for k, v in inputs.items()}

    def rows(w):
        k = w.shape[0] // 128
        return _np.ascontiguousarray(w.reshape(k, 128, -1).transpose(1, 0, 2))

    arrays = dict(constants())
    arrays["x"] = g["attn_a_x"]
    arrays["qkv0"] = rows(g["attn_a_w_qkv"])
    arrays["qkv1"] = rows(_np.concatenate([g[f"attn_b_w_a{n}"].reshape(D, 1024) for n in "qkv"], axis=1))
    arrays["wo0"] = rows(g["attn_a_w_out"])
    arrays["wo1"] = rows(g["attn_b_w_ao"].reshape(1024, D))
    arrays["b_out"] = g["attn_a_b_out"]
    arrays["norm_w"] = g["ffn_norm_w"]
    arrays["gate_wT"] = rows(_np.ascontiguousarray(g["ffn_gate_w"].T))
    arrays["gate_b"] = g["ffn_gate_b"]
    m1 = g["ffn_mlp1_w"].reshape(E, HID, 2, D).transpose(0, 2, 1, 3).reshape(E, 2 * HID, 2, 128)
    arrays["w1"] = _np.ascontiguousarray(m1.transpose(3, 0, 2, 1).reshape(128, E, 4 * HID))
    m2 = g["ffn_mlp2_w"].reshape(E, D, 2, 128)
    arrays["w2"] = _np.ascontiguousarray(m2.transpose(3, 0, 2, 1))
    b1 = g["ffn_mlp1_b"].reshape(E, HID, 2).transpose(0, 2, 1).reshape(-1)
    arrays["mlp_b"] = _np.concatenate([b1, g["ffn_mlp2_b"].reshape(-1)]).reshape(1, -1)

    nc = _bacc.Bacc("TRN2", target_bir_lowering=False, num_devices=1)
    t, feed = {}, {}
    for name, a in arrays.items():
        a = _np.ascontiguousarray(a)
        feed[f"in_{name}"] = a
        t[name] = nc.dram_tensor(f"in_{name}", a.shape, _mybir.dt.from_np(a.dtype), kind="ExternalInput").ap()
    t["out"] = nc.dram_tensor("out_0", (NB, N, D), F32, kind="ExternalOutput").ap()
    t["qkv"] = [t["qkv0"], t["qkv1"]]
    t["wo"] = [t["wo0"], t["wo1"]]
    t["tab"] = [t["c_alibi"], t["c_rope"]]
    program(nc, t)
    r = _run(nc, [feed], core_ids=[0])
    return r.results[0]["out_0"]
```

```python
from contextlib import ExitStack
from math import log2

import numpy as np

import concourse.bass as bass
from concourse import mybir

F32 = mybir.dt.float32
F32R = mybir.dt.float32r
I32 = mybir.dt.int32
U32 = mybir.dt.uint32
ALU = mybir.AluOpType
ACT = mybir.ActivationFunctionType
AX = mybir.AxisListType.X

NB, N, D = 8, 512, 256
TT = N // 128
NT = NB * TT
E, HID = 8, 256
NS = 2 * NT + E - 1
NSP = 72
WIDE = 1280
OFF = [0, 128, 384, 768]
PTO = [0, 512, 1024, 896]
LIMIT, ALPHA = 7.0, 1.702

C_ID, C_IOTA, C_TRI, C_P, C_TOK, C_I8 = 0, 128, 256, 384, 385, 417
C_N = 432


class Sem:

    def __init__(self, h, step):
        self.h, self.step, self.n = h, step, 0

    def tick(self):
        self.n += self.step
        return (self, self.n)


class Queue:

    def __init__(self):
        self.items, self.waited = [], {}

    def wait(self, *tokens):
        for t in tokens:
            if t is None:
                continue
            if isinstance(t, list):
                self.wait(*t)
                continue
            s, v = t
            if self.waited.get(id(s), 0) < v:
                self.waited[id(s)] = v
                self.items.append(lambda e, s=s, v=v: e.wait_ge(s.h, v))

    def go(self, fn, *tokens, sig=None):
        self.wait(*tokens)
        if sig is None:
            self.items.append(fn)
            return None
        t = sig.tick()
        self.items.append(lambda e: fn(e).then_inc(sig.h, sig.step))
        return t

    def play(self, e):
        for f in self.items:
            f(e)


def program(nc, T):
    ctx = ExitStack()
    PE, AC, DV, PO, SP = Queue(), Queue(), Queue(), Queue(), Queue()
    sems = {}

    def S(name, step=1):
        if name not in sems:
            sems[name] = Sem(ctx.enter_context(nc.semaphore(name)), step)
        return sems[name]

    def dma(dst, src, name, *tokens):
        return SP.go(lambda e: e.dma_start(dst, src), *tokens, sig=S(name, 16))

    def dram(name, shape):
        return nc.dram_tensor(name, shape, F32).ap()

    with ctx:
        def sb(name, shape, dt=F32, c=ctx):
            return c.enter_context(nc.sbuf_tensor(name, shape, dt))

        bank = [ctx.enter_context(nc.psum_tensor(f"bank{i}", [128, 512], F32)) for i in range(8)]
        hD = [dram(f"hD{i}", [NT * 128, D]) for i in range(2)]
        rD = [dram(f"rD{i}", [NT * 128, D]) for i in range(2)]
        yD = [dram(f"yD{i}", [NS * 128, D]) for i in range(2)]

        bD = dram("bD", [2, E * 768])
        cst = sb("cst", [128, C_N])
        ident = cst[:, C_ID:C_ID + 128]
        bout = sb("bout", [128, D])
        nw = sb("nw", [128, D])
        gw = sb("gw", [128, 2, E])
        gb = sb("gb", [128, E])
        mhalf = sb("mhalf", [128, TT])
        stage = sb("stage", [128, 2, 512])
        base = nc.sbuf_base
        with ExitStack() as over:
            Wh = sb("Wh", [128, 2, 3072], F32R, over)
            Wl = sb("Wl", [128, 2, 3072], F32R, over)
        assert nc.sbuf_base == base
        Wraw = sb("Wraw", [128, 12288])
        raw1 = Wraw[:, 0:8192].rearrange("p (x n) -> p x n", x=E)
        raw2 = Wraw[:, 8192:12288]
        WO = sb("WO", [128, 8, D])
        M1 = sb("M1", [128, NT, E])
        M2 = sb("M2", [128, NT, E])
        bh = sb("bh", [128, 48], F32R)
        bl = sb("bl", [128, 48], F32R)
        w1 = sb("w1", [128, NT])
        w2 = sb("w2", [128, NT])
        dI = sb("dI", [128, 2, NT], I32)
        idx = sb("idx", [128, NSP], I32)
        etab = sb("etab", [1, NSP], I32)

        t_cst = [dma(cst[:], T["c_cst"], "d_cst"), dma(bout[:], T["b_out"].partition_broadcast(128), "d_cst"),
                 dma(nw[:], T["norm_w"].partition_broadcast(128), "d_cst"),
                 dma(gw[:], T["gate_wT"], "d_cst"), dma(gb[:], T["gate_b"].partition_broadcast(128), "d_cst")]
        t_cst = t_cst[-1]
        t_mh = DV.go(lambda e: e.memset(mhalf[:], -0.5), sig=S("v_mh"))
        for q in (PE, AC, DV, PO):
            q.wait(t_cst)
        PO.wait(t_mh)

        braw = stage[:, 0, 0:48]
        t = dma(braw, T["mlp_b"], "d_b0")
        t_bh = AC.go(lambda e: e.copy(bh[:], braw), t, sig=S("a_bh"))
        t_bl = DV.go(lambda e: e.tensor_tensor(bl[:], braw, bh[:].bitcast(F32), ALU.subtract), t_bh, sig=S("v_bl"))
        dma(bD[0].rearrange("(p n) -> p n", p=128), bh[:].bitcast(F32), "d_b1", t_bh)
        t_bD = dma(bD[1].rearrange("(p n) -> p n", p=128), bl[:].bitcast(F32), "d_b1", t_bl)

        st_free = [[t_bh, t_bl], None]
        wsplit, t_raw, wo_free = {}, {}, {}

        def load_raw(ph, last_proj):
            return [[dma(raw1[:, 4 * i:4 * i + 4], T["w1"][:, 4 * i:4 * i + 4], f"d_raw{ph}{i}", last_proj)
                     for i in range(2)], dma(raw2, T["w2"].rearrange("p x k n -> p (x k n)"), f"d_raw{ph}2", last_proj)]


        def split_weights(ph, slots, free, extra):
            n = 0
            for c in (0, 2, 4, 1, 3, 5):
                cs = slice(c * 512, (c + 1) * 512)
                for kc in range(2):
                    k = n % len(slots)
                    n += 1
                    t = dma(slots[k], T["qkv"][ph][:, kc, cs], f"d_st{ph}_{k}", free[k], extra)
                    a = AC.go(lambda e, k=k, kc=kc, cs=cs: e.copy(Wh[:, kc, cs], slots[k]), t, extra, sig=S("a_whi"))
                    b = DV.go(lambda e, k=k, kc=kc, cs=cs: e.tensor_tensor(
                        Wl[:, kc, cs], slots[k], Wh[:, kc, cs].bitcast(F32), ALU.subtract), a, t, extra, sig=S("v_wlo"))
                    free[k] = [a, b]
                    wsplit[(ph, c)] = [a, b]
                    yield

        def attention(ph, start, t_prev):
            A = ph == 0
            HU = 2 if A else 1
            KD = 64 if A else 128
            NU = NB * 8
            c = ExitStack()

            def b(name, shape, dt=F32):
                return sb(f"{name}_{ph}", shape, dt, c)

            with c:
                tab = b("tab", [128, 16, 512]) if A else b("tab", [128, 3, 512])
                NX = 2 if A else 3
                X = b("X", [128, NX, TT, D])
                xn = b("xn", [128, TT, D])
                xTh = b("xTh", [128, 2, 512], F32R)
                xTl = b("xTl", [128, 2, 512], F32R)
                Qh, Ql, Kh, Kl = (b(f"q{i}", [128, 2, 512], F32R) for i in range(4))
                V = b("V", [128, 2, TT, 512])
                NP = 3 if A else 2
                P = b("P", [128, NP, WIDE])
                PT = b("PT", [128, 2, WIDE])
                OT = b("OT", [128, 8, 512])
                mx = b("mx", [128, NP, 4])
                nm = b("nm", [128, NP, 4])
                rs = b("rs", [128, NP, 4])
                rc = b("rc", [128, NP, 4])
                sts = b("st", [128, 2, TT, 6])
                mvs = b("mv", [128, 2, TT, 2])
                ves = b("ve", [128, 2, TT])
                rstds = b("rstd", [128, 2, TT])
                xs = b("xs", [128, TT, D])
                hh = b("hh", [128, TT, D])
                hT = b("hT", [128, 2, 512])
                ss = b("ss", [128, TT])
                r2 = b("r2", [128, TT])
                lg = b("lg", [128, TT, E])
                v8 = b("v8", [128, TT, E])
                i8 = b("i8", [128, TT, E], U32)
                if8 = b("if8", [128, TT, E])
                dv = b("dv", [128, TT])
                if A:
                    xl = xn
                else:
                    xl = b("xl", [128, TT, D])
                    rp = b("rp", [128, 2, 2, 512])
                    rf = b("rf", [128, 2, 512])
                    yg = b("yg", [128, 4, 2, D])

                jobs = []
                k0 = dma(X[:, 0], T["x"][0].rearrange("(t p) d -> p t d", p=128), "d_x0") if A else None
                if A:
                    for _ in split_weights(0, [OT[:, i] for i in range(8)], [None] * 8, None):
                        pass
                    wo_free[0] = dma(WO[:], T["wo"][0], "d_wo0")
                t_wo = wo_free[0]
                t_tab = [dma(tab[:], T["tab"][ph], "d_tab", start)]
                if start:
                    for q in (PE, AC, DV, PO):
                        q.wait(start)

                t_x, t_xT, xT_used = {}, {}, [None]
                t_q, t_v, qk_used, v_used = {}, {}, {}, {}
                p_ready, p_exp, p_used = {}, {}, {}
                pt_ready, pt_used, ot_used = {}, {}, {}
                bank_free = {i: None for i in range(8)}
                t_y, t_xpre = {}, {}
                B_Q, B_S, B_T, B_O, B_M = (0, 1), (2, 3), (4, 5), 6, 7
                cnt = {"s": 0, "t": 0}

                def tick(n=1):
                    while jobs and n:
                        n -= 1
                        if next(jobs[0], jobs) is jobs:
                            jobs.pop(0)

                def need(what, key):
                    while key not in what:
                        tick()

                def load_x(bt):
                    k = bt % NX
                    free = t_y.get(bt - NX)
                    if A and bt == 0:
                        t_x[bt] = k0
                        return
                    if A:
                        t_x[bt] = dma(X[:, k], T["x"][bt].rearrange("(t p) d -> p t d", p=128), f"d_x{k}", free)
                        return
                    prev = rD[0].rearrange("(b t p) d -> b p t d", p=128, t=TT)
                    tx = dma(X[:, k], prev[bt], f"d_x{k}", free)
                    for t in range(TT):
                        g = bt * TT + t
                        yield
                        a = DV.go(lambda e, k=k, t=t, g=g: e.scalar_tensor_tensor(
                            X[:, k, t], yg[:, t, 0], w1[:, g:g + 1], X[:, k, t], ALU.mult, ALU.add), tx, t_yg[g],
                            sig=S("v_cb"))
                        yg_free[t] = DV.go(lambda e, k=k, t=t, g=g: e.scalar_tensor_tensor(
                            X[:, k, t], yg[:, t, 1], w2[:, g:g + 1], X[:, k, t], ALU.mult, ALU.add), a, sig=S("v_cb"))
                    t_x[bt] = yg_free[TT - 1]

                t_yg, yg_free = {}, [None] * TT

                def gather_y(bt):
                    for t in range(TT):
                        g = bt * TT + t
                        for j in range(2):
                            t_yg[g] = PO.go(lambda e, t=t, j=j, g=g: e.indirect_dma_start(
                                yg[:, t, j, :], None, yD[0], bass.IndirectOffsetOnAxis(ap=dI[:, j, g:g + 1], axis=0)),
                                yg_free[t], t_prev, sig=S(f"d_yg{t}", 16))
                            yield
                            if bt:
                                yield

                def norm(w, src, dst, ready, free):
                    st, mv, ve, rstd = sts[:, w], mvs[:, w], ves[:, w], rstds[:, w]
                    ts = None
                    for t in range(TT):
                        ts = DV.go(lambda e, t=t: e.bn_stats(st[:, t], src(t)), ready, sig=S("v_st"))
                        if t % 2:
                            yield
                    for t in range(TT):
                        ta = DV.go(lambda e, t=t: e.bn_aggr(mv[:, t], st[:, t]), ts, sig=S("v_ag"))
                    tp = PO.go(lambda e: e.tensor_scalar(ve, mv[:, :, 1], 1e-5, None, ALU.add), ta, sig=S("p_ve"))
                    tp = PO.go(lambda e: e.tensor_tensor(rstd, ve, mhalf[:], ALU.pow), tp, sig=S("p_rs"))
                    for _ in range(5 if A else 4):
                        yield
                    for t in range(TT):
                        tn = DV.go(lambda e, t=t: e.tensor_scalar(dst[:, t], src(t), mv[:, t, 0:1], rstd[:, t:t + 1],
                                                                  ALU.subtract, ALU.mult), tp, free, sig=S("v_xn"))
                        if t % 2:
                            yield
                    return tn

                t_xn, xn_used, xl_used = {}, [None], [None]

                def pre(bt):
                    k = bt % NX
                    tn = yield from norm(0, lambda t: X[:, k, t], xn, t_x[bt], xn_used[0])
                    t_xpre[bt] = tn
                    if A:
                        for t in range(TT):
                            t_xpre[bt] = PO.go(lambda e, t=t: e.tensor_tensor(X[:, k, t], X[:, k, t], bout[:], ALU.add),
                                               tn, sig=S("p_xb"))
                    t_xn[bt] = tn

                def transpose4(src, kc, ready):
                    for t in range(TT):
                        tp = PE.go(lambda e, t=t: e.transpose(bank[B_M][:, t * 128:(t + 1) * 128],
                                                             src[:, t, kc * 128:(kc + 1) * 128], ident),
                                   ready, bank_free[B_M], sig=S("m_tr") if t == TT - 1 else None)
                    return tp

                def xpose(bt, kc):
                    need(t_xn, bt)
                    tp = transpose4(xn, kc, t_xn[bt])
                    if kc == 1:
                        xn_used[0] = tp
                    a = AC.go(lambda e: e.copy(xTh[:, kc], bank[B_M][:]), tp, xT_used[0], sig=S("a_xT"))
                    v = DV.go(lambda e: e.tensor_tensor(xTl[:, kc], bank[B_M][:], xTh[:, kc].bitcast(F32),
                                                        ALU.subtract), a, xT_used[0], sig=S("v_xT"))
                    bank_free[B_M] = [v]
                    t_xT[bt] = [a, v]

                def mm3(out, lh, ll, rh, rl, first, last, sig, *tok):
                    PE.go(lambda e: e.matmul(out, lh, rh, start=first, stop=False), *tok)
                    PE.go(lambda e: e.matmul(out, lh, rl, start=False, stop=False))
                    return PE.go(lambda e: e.matmul(out, ll, rh, start=False, stop=last), sig=sig if last else None)

                def proj_v(u, ts4):
                    bt, p = divmod(u, 8)
                    g = u // 4
                    vk = g % 2
                    c0 = 2048 + (p // 4) * 512
                    for t in ts4:
                        bk = bank[B_Q[t % 2]]
                        ts = slice(t * 128, (t + 1) * 128)
                        for kc in range(2):
                            tp = mm3(bk[:], xTh[:, kc, ts], xTl[:, kc, ts], Wh[:, kc, c0:c0 + 512],
                                     Wl[:, kc, c0:c0 + 512], kc == 0, kc == 1, S("m_v"), wsplit[(ph, 4 + p // 4)], t_xT[bt],
                                     bank_free[B_Q[t % 2]])
                        if A:
                            a = DV.go(lambda e, t=t, bk=bk: e.tensor_copy(V[:, vk, t], bk[:]), tp, v_used.get(g - 2),
                                      sig=S("v_v"))
                        else:
                            a = AC.go(lambda e, t=t, bk=bk: e.copy(V[:, vk, t], bk[:]), tp, v_used.get(g - 2),
                                      sig=S("a_v"))
                        bank_free[B_Q[t % 2]] = [a]
                        t_v.setdefault(g, []).append(a)
                    xT_used[0] = tp

                def proj_qk(u, j):
                    bt, p = divmod(u, 8)
                    k = u % 2
                    H, L = ((Qh, Ql), (Kh, Kl))[j]
                    bk = bank[B_Q[j]]
                    c0 = j * 1024 + p * 128
                    for kc in range(2):
                        tp = mm3(bk[:], Wh[:, kc, c0:c0 + 128], Wl[:, kc, c0:c0 + 128], xTh[:, kc], xTl[:, kc],
                                 kc == 0, kc == 1, S("m_qk"), wsplit[(ph, 2 * j + p // 4)], t_xT[bt], bank_free[B_Q[j]])
                    xT_used[0] = tp
                    used = qk_used.get(u - 2)
                    t_q.setdefault(u, [])
                    if A:
                        a = AC.go(lambda e: e.copy(H[:, k], bk[:]), tp, used, sig=S("a_qk"))

                        def low():
                            v = DV.go(lambda e: e.tensor_tensor(L[:, k], bk[:], H[:, k].bitcast(F32), ALU.subtract), a,
                                      used, sig=S("v_qk"))
                            bank_free[B_Q[j]] = [v]
                            t_q[u].extend([a, v])
                        lows.append(low)
                        return
                    rj = rp[:, j]
                    DV.go(lambda e: e.tensor_tensor(rj[:, 0], bk[:], tab[:, 1], ALU.mult), tp, rope_free[j], sig=S("v_rp"))
                    DV.go(lambda e: e.tensor_tensor(rj[0:64, 1], bk[64:128, :], tab[64:128, 2], ALU.mult), sig=S("v_rp"))
                    v = DV.go(lambda e: e.tensor_tensor(rj[64:128, 1], bk[0:64, :], tab[0:64, 2], ALU.mult),
                              sig=S("v_rp"))
                    bank_free[B_Q[j]] = [v]
                    g = PO.go(lambda e: e.tensor_tensor(rf[:, j], rj[:, 0], rj[:, 1], ALU.add), v, rf_free[j],
                              sig=S("p_rf"))
                    rope_free[j] = rope_done[j] = g

                def proj(u, early=lambda: None):
                    if u % 4 == 0:
                        early()
                        proj_v(u, range(TT))
                    proj_qk(u, 0)
                    if u % 4:
                        early()
                    proj_qk(u, 1)

                rope_done = [None, None]

                def rope_split(u):
                    k = u % 2
                    for j, (H, L) in enumerate(((Qh, Ql), (Kh, Kl))):
                        used = qk_used.get(u - 2)
                        a = AC.go(lambda e, H=H, j=j: e.copy(H[:, k], rf[:, j]), rope_done[j], used, sig=S("a_qk"))
                        l = PO.go(lambda e, H=H, L=L, j=j: e.tensor_tensor(
                            L[:, k], rf[:, j], H[:, k].bitcast(F32), ALU.subtract), a, used, sig=S("p_lo"))
                        rf_free[j] = [a, l]
                        t_q[u] += [a, l]

                rope_free, rf_free = [None, None], [None, None]

                def scores(h, between=()):
                    between = list(between)
                    u, hl = divmod(h, HU)
                    k = u % 2
                    r = slice(64 * hl, 64 * hl + 64) if A else slice(0, 128)
                    pb = h % NP
                    tb = tab[:, h % 16] if A else tab[:, 0]
                    for t in reversed(range(TT)):
                        s = B_S[cnt["s"] % 2]
                        cnt["s"] += 1
                        w = (t + 1) * 128
                        ts = slice(t * 128, w)
                        tp = mm3(bank[s][:, 0:w], Qh[r, k, ts], Ql[r, k, ts], Kh[r, k, 0:w], Kl[r, k, 0:w],
                                 True, True, S("m_s"), t_q[u], bank_free[s])
                        v = DV.go(lambda e, s=s, w=w, t=t: e.tensor_tensor_reduce(
                            out=P[:, pb, OFF[t]:OFF[t] + w], in0=bank[s][:, 0:w], in1=tb[:, 512 - w:512], scale=1.0,
                            scalar=-3e38, op0=ALU.add, op1=ALU.max, accum_out=mx[:, pb, t:t + 1]),
                            tp, t_tab, p_used.get(h - NP), sig=S("v_mx"))
                        bank_free[s] = [v]
                        if lows and h > 1 and t == 1:
                            lows.pop(0)()
                        if between:
                            between.pop(0)()
                        tick()
                    qk_used[u] = tp
                    sc = 0.125 if A else 1.0 / 128
                    t_nm[h] = DV.go(lambda e: e.tensor_scalar(nm[:, pb], mx[:, pb], -sc, None, ALU.mult), v, sig=S("v_nm"))

                t_nm, lows = {}, []

                def exps(h):
                    pb = h % NP
                    sc = 0.125 if A else 1.0 / 128
                    for t in range(TT):
                        ps = P[:, pb, OFF[t]:OFF[t] + (t + 1) * 128]
                        a = AC.go(lambda e, ps=ps, t=t: e.activation(ps, ps, ACT.Exp, bias=nm[:, pb, t:t + 1], scale=sc,
                                                                     accum_out=rs[:, pb, t:t + 1]), t_nm[h], sig=S("a_exp"))
                    p_exp[h] = a

                def scale(h):
                    pb = h % NP
                    r = DV.go(lambda e: e.reciprocal(rc[:, pb], rs[:, pb]), p_exp[h], sig=S("v_rc"))
                    for t in range(TT):
                        ps = P[:, pb, OFF[t]:OFF[t] + (t + 1) * 128]
                        v = DV.go(lambda e, ps=ps, t=t: e.tensor_scalar(ps, ps, rc[:, pb, t:t + 1], None, ALU.mult),
                                  r, sig=S("v_sc"))
                    p_ready[h] = v

                def flip(h):
                    pb = h % NP
                    pt = h % 2
                    pt_ready[h] = []

                    def part(cs):
                        s = B_T[cnt["t"] % 2]
                        cnt["t"] += 1
                        at = 0
                        for cc in cs:
                            for t in range(cc, TT):
                                lastone = cc == cs[-1] and t == TT - 1
                                tp = PE.go(lambda e, at=at, s=s, t=t, cc=cc: e.transpose(
                                    bank[s][:, at:at + 128], P[:, pb, OFF[t] + cc * 128:OFF[t] + cc * 128 + 128], ident),
                                    p_ready[h], bank_free[s], sig=S("m_t") if lastone else None)
                                at += 128
                        dst = PT[:, pt, PTO[cs[0]]:PTO[cs[0]] + at]
                        x = AC.go(lambda e: e.copy(dst, bank[s][:, 0:at]), tp, pt_used.get(h - 2), sig=S("a_pt"))
                        bank_free[s] = [x]
                        p_used[h] = tp
                        pt_ready[h].append(x)
                    return [lambda cs=cs: part(cs) for cs in ((0,), (1, 3), (2,))]

                def attend(u):
                    bt, p = divmod(u, 8)
                    g = u // 4
                    vk = g % 2
                    o = bank[B_O]
                    for cc in range(TT):
                        for hl in range(HU):
                            h = u * HU + hl
                            col = (u % 4) * 128 + hl * 64
                            w = 512 - cc * 128
                            out = o[64 * hl:64 * hl + 64, cc * 128:512] if A else o[:, cc * 128:512]
                            lastone = cc == TT - 1 and hl == HU - 1
                            tp = PE.go(lambda e, out=out, cc=cc, col=col, h=h, w=w: e.matmul(
                                out, V[:, vk, cc, col:col + KD], PT[:, h % 2, PTO[cc]:PTO[cc] + w],
                                start=cc == 0, stop=cc == TT - 1), pt_ready[h], t_v[g], bank_free[B_O],
                                sig=S("m_o") if lastone else None)
                    for hl in range(HU):
                        pt_used[u * HU + hl] = tp
                    if u % 4 == 3:
                        v_used[g] = tp
                    a = AC.go(lambda e: e.copy(OT[:, p], o[:]), tp, ot_used.get(bt - 1), sig=S("a_o"))
                    bank_free[B_O] = [a]
                    if p == 7:
                        t_ot[bt] = a

                t_ot = {}
                t_x1 = {}

                def outproj(bt, half):
                    for t2 in range(2):
                        t = half * 2 + t2
                        for ch in range(8):
                            tp = PE.go(lambda e, t=t, t2=t2, ch=ch: e.matmul(
                                bank[B_M][:, t2 * 256:t2 * 256 + 256], OT[:, ch, t * 128:(t + 1) * 128], WO[:, ch],
                                start=ch == 0, stop=ch == 7), t_ot[bt], t_wo, bank_free[B_M],
                                sig=S("m_y") if t2 == 1 and ch == 7 else None)
                    if half == 1:
                        ot_used[bt] = tp

                    add_x(bt, half, tp)

                def add_x(bt, half, tp):
                    k = bt % NX
                    v = DV.go(lambda e: e.tensor_tensor(X[:, k, 2 * half:2 * half + 2], bank[B_M][:].rearrange(
                        "p (t d) -> p t d", t=2), X[:, k, 2 * half:2 * half + 2], ALU.add), tp, t_xpre[bt], sig=S("v_x1"))
                    bank_free[B_M] = [v]
                    if half:
                        t_x1[bt] = v

                hold = {"hh": None, "xs": None, "xl": None, "hT": None, "lg": None}
                t_hh = {}

                def gate_norm(bt):
                    k = bt % NX
                    tn = yield from norm(1, lambda t: X[:, k, t], xl, t_x1[bt], (xn_used if A else xl_used)[0])
                    for t in range(TT):
                        ta = AC.go(lambda e, t=t: e.activation(xs[:, t], xl[:, t], ACT.Square,
                                                               accum_out=ss[:, t:t + 1]), tn, hold["xs"], sig=S("a_ss"))
                    tg = PO.go(lambda e: e.tensor_scalar(ves[:, 1], ss[:], 1.0 / D, float(np.finfo(np.float32).eps),
                                                         ALU.mult, ALU.add), ta, sig=S("p_v2"))
                    tg = PO.go(lambda e: e.tensor_tensor(r2[:], ves[:, 1], mhalf[:], ALU.pow), tg, sig=S("p_r2"))
                    for _ in range(6 if A else 3):
                        yield
                    yield
                    for t in range(TT):
                        th = DV.go(lambda e, t=t: e.scalar_tensor_tensor(hh[:, t], xl[:, t], r2[:, t:t + 1], nw[:],
                                                                         ALU.mult, ALU.mult), tg, hold["hh"], sig=S("v_h"))
                        if t % 2:
                            yield
                    tx = PO.go(lambda e: e.tensor_tensor(xs[:], X[:, k], xl[:], ALU.add), ta, tn, sig=S("p_xs"))
                    (xn_used if A else xl_used)[0] = [th, tx]
                    t_y[bt] = [tx]
                    dh = dma(hD[ph].rearrange("(b t p) d -> b p t d", p=128, t=TT)[bt], hh[:], "d_h", th)
                    dx = dma(rD[ph].rearrange("(b t p) d -> b p t d", p=128, t=TT)[bt], xs[:], "d_r", tx)
                    hold["xs"] = [dx]
                    hold["hh"] = [dh]
                    t_hh[bt] = th

                t_hT = {}

                def gate_flip(bt, kc):
                    need(t_hh, bt)
                    tp = transpose4(hh, kc, t_hh[bt])
                    a = AC.go(lambda e: e.copy(hT[:, kc], bank[B_M][:]), tp, hold["hT"], sig=S("a_hT"))
                    bank_free[B_M] = [a]
                    t_hT[bt] = a
                    if kc == 1:
                        hold["hh"] = hold["hh"] + [tp]

                def gate_top(bt):
                    for t in range(TT):
                        for kc in range(2):
                            tp = PE.go(lambda e, t=t, kc=kc: e.matmul(
                                bank[B_M][:, t * E:(t + 1) * E], hT[:, kc, t * 128:(t + 1) * 128], gw[:, kc],
                                start=kc == 0, stop=kc == 1), t_hT[bt], bank_free[B_M],
                                sig=S("m_lg") if t == TT - 1 and kc == 1 else None)
                    hold["hT"] = tp
                    v = DV.go(lambda e: e.tensor_tensor(lg[:], bank[B_M][:, 0:TT * E].rearrange("p (t k) -> p t k", k=E),
                                                        gb[:].rearrange("p (a k) -> p a k", a=1).broadcast_to(
                                                            [128, TT, E]), ALU.add), tp, hold["lg"], sig=S("v_lg"))
                    bank_free[B_M] = [v]
                    jobs.insert(0, top(bt, v))

                def top(bt, v):
                    yield
                    for t in range(TT):
                        v1 = DV.go(lambda e, t=t: e.max(v8[:, t], lg[:, t]), v, sig=S("v_m8"))
                    yield
                    for t in range(TT):
                        v2 = DV.go(lambda e, t=t: e.max_index(i8[:, t], v8[:, t], lg[:, t]), v1, sig=S("v_i8"))
                    yield
                    v2 = DV.go(lambda e: e.tensor_copy(if8[:], i8[:]), v2, sig=S("v_if"))
                    v3 = DV.go(lambda e: e.tensor_tensor(dv[:], v8[:, :, 1], v8[:, :, 0], ALU.subtract), v1, sig=S("v_dv"))
                    g0 = bt * TT
                    io = cst[:, C_I8:C_I8 + E].rearrange("p (a k) -> p a k", a=1).broadcast_to([128, TT, E])
                    for j, M in enumerate((M1, M2)):
                        m = DV.go(lambda e, j=j, M=M: e.tensor_tensor(
                            M[:, g0:g0 + TT], io, if8[:, :, j:j + 1].broadcast_to([128, TT, E]), ALU.is_equal),
                            v2, sig=S("v_M"))
                    a = AC.go(lambda e: e.activation(dv[:], dv[:], ACT.Exp), v3, sig=S("a_ev"))
                    yield
                    yield
                    v4 = DV.go(lambda e: e.tensor_scalar(w1[:, g0:g0 + TT], dv[:], 1.0, None, ALU.add), a, sig=S("v_w"))
                    v5 = DV.go(lambda e: e.reciprocal(w1[:, g0:g0 + TT], w1[:, g0:g0 + TT]), v4, sig=S("v_w"))
                    v6 = DV.go(lambda e: e.tensor_tensor(w2[:, g0:g0 + TT], w1[:, g0:g0 + TT], dv[:], ALU.mult), v5,
                               sig=S("v_w"))
                    hold["lg"] = v6
                    t_M[bt] = m
                t_M = {}

                if not A:
                    jobs.append(gather_y(0))
                jobs.append(load_x(0))
                jobs.append(pre(0))
                xpose(0, 0)
                xpose(0, 1)
                proj(0)
                if not A:
                    rope_split(0)
                while lows:
                    lows.pop(0)()
                for h in range(HU):
                    scores(h)
                    exps(h)
                proj(1)
                while lows:
                    lows.pop(0)()
                if A:
                    proj_qk(2, 0)
                if not A:
                    rope_split(1)
                for h in range(HU):
                    scale(h)
                PF = 2 if A else 3
                for u in range(NU):
                    bt, p = divmod(u, 8)
                    nx = bt + 1 < NB
                    if A and p == 2 and nx:
                        jobs.append(load_x(bt + 1))
                    if not A and p == 0:
                        if bt >= 1:
                            outproj(bt - 1, 0)
                    for hl in range(HU):
                        h = u * HU + hl
                        n = h + HU
                        more = [lambda: xpose(bt + 1, 1)] if A and p == 5 and hl == 1 and nx else []
                        if n < NU * HU:
                            fl = flip(h)
                            scores(n, fl[:1] + more + fl[1:])
                        else:
                            for f in flip(h):
                                f()
                        if not A and u >= 1 and u + 2 < NU:
                            rope_split(u + 2)
                        if n < NU * HU:
                            exps(n)
                        if A and HU <= n - 1 < NU * HU:
                            scale(n - 1)
                        if A and u % 4 == 2 and u + 2 < NU:
                            proj_v(u + 2, (2 * hl, 2 * hl + 1))
                        if A and u + 2 + hl < NU:
                            proj_qk(u + 2 + hl, 1 - hl)
                        if A and p == 5 and hl == 0 and nx:
                            xpose(bt + 1, 0)
                        if A and p == 0 and bt >= 1:
                            outproj(bt - 1, hl)
                        if A and p == PF and bt >= 1 and hl == 0:
                            gate_flip(bt - 1, 0)
                    if not A and p == 0 and bt >= 1:
                        outproj(bt - 1, 1)
                    if p == 0 and bt >= 1:
                        jobs.insert(0, gate_norm(bt - 1))
                    if not A and u == 0:
                        jobs += [gather_y(1), load_x(1), pre(1)]
                    if not A and bt >= 1 and p == PF:
                        gate_flip(bt - 1, 0)
                    if u == 0 and not A:
                        proj(2)
                        rope_split(2)
                    early = (lambda: scale(n)) if not A and n < NU * HU else (lambda: None)
                    if A:
                        pass
                    elif u + 3 < NU:
                        proj(u + 3, early)
                    else:
                        early()
                    if bt >= 1:
                        if p == PF:
                            gate_flip(bt - 1, 1)
                        elif p == PF + 1:
                            gate_top(bt - 1)
                    if A and p == 2 and nx:
                        jobs.append(pre(bt + 1))
                    if not A:
                        tick()
                    if not A and p == 4 and nx:
                        xpose(bt + 1, 0)
                    if u == (NU - 3 if A else NU - 4):
                        t_raw[ph] = load_raw(ph, xT_used[0])
                    tick()
                    attend(u)
                    tick()
                    if not A and p == 4 and nx:
                        xpose(bt + 1, 1)
                    if not A and p == 5 and bt + 2 < NB:
                        jobs += [gather_y(bt + 2), load_x(bt + 2), pre(bt + 2)]
                bt = NB - 1
                outproj(bt, 0)
                outproj(bt, 1)
                jobs.append(gate_norm(bt))
                gate_flip(bt, 0)
                gate_flip(bt, 1)
                gate_top(bt)
                need(t_M, bt)
                t_M = t_M[bt]
            ends = [S(n) for n in sems if n[0] in "mavpd"]
            return [(s, s.n) for s in ends if s.n], t_M

        def experts(ph, t_end, t_M, last):
            c = ExitStack()

            def b(name, shape, dt=F32):
                return sb(f"{name}f_{ph}", shape, dt, c)

            with c:
                W1h = b("W1h", [128, E, 2, 512], F32R)
                W1l = b("W1l", [128, E, 2, 512], F32R)
                W2 = b("W2", [128, E, 2, D])
                BR = b("BR", [2, E * 768], F32R)
                on2 = b("on2", [2, 128], F32R)
                Ms = b("Ms", [128, NT, E])
                Tt = b("Tt", [128, NT, E])
                inc = b("inc", [128, NT, E])
                tmp = b("tmp", [128, NT, E])
                tm2 = b("tm2", [128, NT, E])
                one = b("one", [128, NT])
                n8 = b("n8", [128, 4, E])
                ni = b("ni", [128, E], I32)
                dF = b("dF", [128, 2, NT])
                ia = b("ia", [128, 2, NT], I32)
                fa = b("fa", [128, 2, NT])
                fb = b("fb", [128, 2, NT])
                ob = b("ob", [128, 4, 128], F32R)
                oa = b("oa", [128, 4, NSP], F32R)
                se = b("se", [1, NSP, E])
                ef = b("ef", [1, NSP])
                G = b("G", [128, 4, D])
                XTh = b("XTh", [128, 2, 2, 128], F32R)
                XTl = b("XTl", [128, 2, 2, 128], F32R)
                gl = b("gl", [128, 2, HID])
                li = b("li", [128, 2, HID])
                sg = b("sg", [128, 2, HID])
                ac = b("ac", [128, 2, HID])
                AT = b("AT", [128, 2, 2, 128])
                Y = b("Y", [128, 2, D])
                for q in (PE, AC, DV, PO, SP):
                    q.wait(t_end)

                v = DV.go(lambda e: e.tensor_tensor(Ms[:], M1[:], M2[:], ALU.add), t_M, sig=S("r_v"))
                flat = Ms[:].rearrange("p t k -> p (t k)")
                ones = b("ones", [128, 128])
                vo = DV.go(lambda e: e.memset(ones[:], 1.0), sig=S("r_v"))
                von = DV.go(lambda e: e.memset(one[:], 1.0), sig=S("r_v"))
                PE.go(lambda e: e.matmul(bank[0][:, 0:256], cst[:, C_TRI:C_TRI + 128], flat, start=True, stop=True), v, vo)
                t_rk = PE.go(lambda e: e.matmul(bank[1][:, 0:256], ones[:], flat, start=True, stop=True), sig=S("r_m"))
                v = DV.go(lambda e: e.tensor_copy(Tt[:].rearrange("p t k -> p (t k)"), bank[1][:, 0:256]), t_rk, sig=S("r_v"))
                for k in range(E):
                    vs = DV.go(lambda e, k=k: e.tensor_tensor_scan(inc[:, :, k], one[:], Tt[:, :, k], 0.0,
                                                                  ALU.mult, ALU.add), v, von, sig=S("r_v"))
                v1 = DV.go(lambda e: e.tensor_scalar(n8[:, 0], inc[:, NT - 1], 127.0, None, ALU.add), vs, sig=S("r_v"))
                v1 = DV.go(lambda e: e.tensor_copy(ni[:], n8[:, 0]), v1, sig=S("r_v"))
                v1 = DV.go(lambda e: e.tensor_single_scalar(ni[:], ni[:], 7, ALU.arith_shift_right), v1, sig=S("r_v"))
                v1 = DV.go(lambda e: e.tensor_copy(n8[:, 1], ni[:]), v1, sig=S("r_v"))
                v1 = DV.go(lambda e: e.tensor_tensor_scan(n8[:, 2], one[:, 0:E], n8[:, 1], 0.0, ALU.mult, ALU.add), v1,
                           sig=S("r_v"))
                t_inc = v1
                v1 = DV.go(lambda e: e.tensor_tensor(n8[:, 3], n8[:, 2], n8[:, 1], ALU.subtract), v1, sig=S("r_v"))
                v1 = DV.go(lambda e: e.tensor_scalar(n8[:, 3], n8[:, 3], 128.0, None, ALU.mult), v1, sig=S("r_v"))
                v2 = DV.go(lambda e: e.tensor_tensor(tmp[:], inc[:], Tt[:], ALU.subtract), vs, sig=S("r_v"))
                v2 = DV.go(lambda e: e.tensor_tensor(tmp[:].rearrange("p t k -> p (t k)"), bank[0][:, 0:256],
                                                     tmp[:].rearrange("p t k -> p (t k)"), ALU.add), v2, sig=S("r_v"))
                v2 = DV.go(lambda e: e.tensor_tensor(tmp[:], tmp[:], n8[:, 3:4].broadcast_to([128, NT, E]), ALU.add),
                           v2, v1, sig=S("r_v"))
                for j, M in enumerate((M1, M2)):
                    v3 = DV.go(lambda e, M=M: e.tensor_tensor(tm2[:], M[:], tmp[:], ALU.mult), v2, sig=S("r_v"))
                    v2 = DV.go(lambda e, j=j: e.reduce_sum(dF[:, j], tm2[:], AX), v3, sig=S("r_v"))
                v2 = DV.go(lambda e: e.tensor_copy(dI[:], dF[:]), v2, sig=S("r_v"))
                t_dI = v2
                v2 = DV.go(lambda e: e.tensor_single_scalar(ia[:], dI[:], 7, ALU.arith_shift_right), v2, sig=S("r_v"))
                v2 = DV.go(lambda e: e.tensor_copy(fa[:], ia[:]), v2, sig=S("r_v"))
                v2 = DV.go(lambda e: e.scalar_tensor_tensor(fb[:], fa[:], -128.0, dF[:], ALU.mult, ALU.add), v2, sig=S("r_v"))
                v4 = DV.go(lambda e: e.tensor_tensor(
                    se[:], cst[0:1, C_IOTA:C_IOTA + NSP].rearrange("p (s a) -> p s a", a=1).broadcast_to([1, NSP, E]),
                    n8[0:1, 2:3, :].broadcast_to([1, NSP, E]), ALU.is_ge), t_inc, sig=S("r_v"))
                v4 = DV.go(lambda e: e.reduce_sum(ef[:], se[:], AX), v4, sig=S("r_v"))
                v4 = DV.go(lambda e: e.tensor_scalar(ef[:], ef[:], float(E - 1), None, ALU.min), v4, sig=S("r_v"))
                t_et = DV.go(lambda e: e.tensor_copy(etab[:], ef[:]), v4, sig=S("r_v"))
                ob_free = [None] * 4
                for g in range(2 * NT):
                    t, j = divmod(g, 2)
                    k = g % 4
                    x = DV.go(lambda e, k=k, t=t, j=j: e.tensor_scalar(ob[:, k], cst[:, C_IOTA:C_IOTA + 128],
                                                                       fb[:, j, t:t + 1], None, ALU.is_equal),
                              v2, ob_free[k], sig=S("r_ob"))
                    y = DV.go(lambda e, k=k, t=t, j=j: e.tensor_scalar(
                        oa[:, k], cst[:, C_IOTA:C_IOTA + NSP], fa[:, j, t:t + 1], cst[:, C_TOK + t:C_TOK + t + 1],
                        ALU.is_equal, ALU.mult), v2, ob_free[k], sig=S("r_oa"))
                    ob_free[k] = PE.go(lambda e, k=k, g=g: e.matmul(bank[2][:, 0:NSP], ob[:, k], oa[:, k],
                                                                    start=g == 0, stop=g == 2 * NT - 1), x, y, sig=S("r_id"))
                t_idx = DV.go(lambda e: e.tensor_copy(idx[:], bank[2][:, 0:NSP]), ob_free[k], sig=S("r_v"))

                tbr = dma(BR[:].bitcast(F32), bD, "d_BR")
                von2 = DV.go(lambda e: e.tensor_copy(on2[:], ones[0:2, :]), vo, sig=S("r_v"))
                raw, raw_w2 = t_raw[ph]
                tw = []
                for k in range(E):
                    W1f = [w[:, k].rearrange("p a b -> p (a b)") for w in (W1h, W1l)]
                    a = AC.go(lambda e, k=k, W1f=W1f: e.copy(W1f[0], raw1[:, k]), raw[k // 4], sig=S("a_w1"))
                    g = PO.go(lambda e, k=k, W1f=W1f: e.tensor_tensor(W1f[1], raw1[:, k], W1f[0].bitcast(F32),
                                                                    ALU.subtract), a, raw[k // 4], sig=S("p_w1"))
                    tw = [a, g]
                tw2 = dma(W2[:].rearrange("p x k n -> p (x k n)"), raw2, "d_w2", raw_w2)
                more = iter(()) if last else split_weights(1, [stage[:, i] for i in range(2)], [t_end, t_end], [tw, tw2])

                g_free, t_g = {}, {}
                xt_free, t_xt = {}, {}
                gl_free, t_ac = {}, {}
                at_free, y_free = {}, {}
                bf = {i: [t_idx] for i in range(8)}
                B1, BX, BA, BY = (0, 1), (2, 3), (4, 5), (6, 7)
                y_out = yD[ph].rearrange("(s p) d -> s p d", p=128)
                t_yd = []

                def gather(a):
                    t_g[a] = PO.go(lambda e: e.indirect_dma_start(G[:, a % 4], None, hD[ph], bass.IndirectOffsetOnAxis(
                        ap=idx[:, a:a + 1], axis=0)), t_idx, g_free.get(a - 4), sig=S(f"d_g{a % 4}", 16))

                def flip_x(a):
                    k = a % 2
                    bk = bank[BX[k]]
                    for kc in range(2):
                        tp = PE.go(lambda e, kc=kc: e.transpose(bk[:, kc * 128:(kc + 1) * 128],
                                                               G[:, a % 4, kc * 128:(kc + 1) * 128], ident),
                                   t_g[a], bf[BX[k]], sig=S("f_x") if kc else None)
                    g_free[a] = tp
                    src = bk[:, 0:256].rearrange("p (a b) -> p a b", a=2)
                    x = AC.go(lambda e: e.copy(XTh[:, k], src), tp, xt_free.get(a - 2), sig=S("a_fx"))
                    y = DV.go(lambda e: e.tensor_tensor(XTl[:, k], src, XTh[:, k].bitcast(F32), ALU.subtract), x,
                              xt_free.get(a - 2), sig=S("v_fx"))
                    bf[BX[k]] = [y]
                    t_xt[a] = [x, y]

                def up(a):
                    k = a % 2
                    bk = bank[B1[k]]
                    PE.wait(t_et, tw, tbr, von2, t_xt[a], bf[B1[k]])

                    def f(e):
                        r = e.value_load(etab[0:1, a:a + 1], min_val=0, max_val=E - 1)
                        ex = bass.ds(r, 1)
                        bias = BR[:, 0:E * 512].rearrange("q (x n) -> q x n", x=E)
                        e.matmul(bk[:], on2[:], bias[:, ex].rearrange("q x n -> q (x n)"), start=True, stop=False)
                        for kc in range(2):
                            wh = W1h[:, ex, kc].rearrange("p x n -> p (x n)")
                            wl = W1l[:, ex, kc].rearrange("p x n -> p (x n)")
                            e.matmul(bk[:], XTh[:, k, kc], wh, start=False, stop=False)
                            e.matmul(bk[:], XTh[:, k, kc], wl, start=False, stop=False)
                            i = e.matmul(bk[:], XTl[:, k, kc], wh, start=False, stop=kc == 1)
                        return i
                    tp = PE.go(f, sig=S("f_up"))
                    xt_free[a] = tp
                    g = DV.go(lambda e: e.tensor_scalar(gl[:, k], bk[:, 0:HID], LIMIT, None, ALU.min), tp, gl_free.get(a - 2),
                              sig=S("v_gl"))
                    s = AC.go(lambda e: e.activation(sg[:, k], gl[:, k], ACT.Sigmoid, scale=ALPHA), g, gl_free.get(a - 2),
                              sig=S("a_sg"))
                    l = DV.go(lambda e: e.tensor_scalar(li[:, k], bk[:, HID:2 * HID], LIMIT, -LIMIT, ALU.min, ALU.max), tp,
                              gl_free.get(a - 2), sig=S("v_li"))
                    bf[B1[k]] = [l]
                    m = DV.go(lambda e: e.scalar_tensor_tensor(li[:, k], li[:, k], 1.0, gl[:, k], ALU.add, ALU.mult), l, g,
                              sig=S("v_lg2"))
                    m = DV.go(lambda e: e.tensor_tensor(ac[:, k], li[:, k], sg[:, k], ALU.mult), m, s, at_free.get(a - 2),
                              sig=S("v_ac"))
                    gl_free[a] = m
                    t_ac[a] = m

                t_at = {}

                def flip_a(a):
                    k = a % 2
                    bk = bank[BA[k]]
                    for kc in range(2):
                        tp = PE.go(lambda e, kc=kc: e.transpose(bk[:, kc * 128:(kc + 1) * 128],
                                                               ac[:, k, kc * 128:(kc + 1) * 128], ident),
                                   t_ac[a], bf[BA[k]], sig=S("f_a") if kc else None)
                    at_free[a] = tp
                    src = bk[:, 0:256].rearrange("p (a b) -> p a b", a=2)
                    x = AC.go(lambda e: e.copy(AT[:, k], src), tp, t_dn.get(a - 2), sig=S("a_at"))
                    bf[BA[k]] = [x]
                    t_at[a] = x

                t_dn = {}

                def down(a):
                    k = a % 2
                    bk = bank[BY[k]]
                    PE.wait(tw2, t_at[a], bf[BY[k]])

                    def f(e):
                        r = e.value_load(etab[0:1, a:a + 1], min_val=0, max_val=E - 1)
                        ex = bass.ds(r, 1)
                        bias = BR[:, E * 512:E * 768].rearrange("q (x n) -> q x n", x=E)
                        e.matmul(bk[:, 0:D], on2[:], bias[:, ex].rearrange("q x n -> q (x n)"), start=True, stop=False)
                        for kc in range(2):
                            i = e.matmul(bk[:, 0:D], AT[:, k, kc], W2[:, ex, kc].rearrange("p x n -> p (x n)"),
                                         start=False, stop=kc == 1)
                        return i
                    tp = PE.go(f, sig=S("f_dn"))
                    t_dn[a] = tp
                    x = AC.go(lambda e: e.copy(Y[:, k], bk[:, 0:D]), tp, y_free.get(a - 2), sig=S("a_y"))
                    bf[BY[k]] = [x]
                    y_free[a] = dma(y_out[a], Y[:, k], f"d_y{k}", x)

                for a in range(4):
                    gather(a)
                flip_x(0)
                flip_x(1)
                up(0)
                up(1)
                flip_x(2)
                for a in range(NS):
                    flip_a(a)
                    if a % 4 == 3:
                        next(more, None)
                    if a == 52 and not last:
                        wo_free[0] = dma(WO[:], T["wo"][1], "d_wo1")
                    if a + 3 < NS:
                        flip_x(a + 3)
                    if a + 4 < NS:
                        gather(a + 4)
                    if a + 2 < NS:
                        up(a + 2)
                    down(a)
                t_yd = [y_free[NS - 1], y_free[NS - 2]]

                if last:
                    yg = WO[:].rearrange("p (s j) d -> p s j d", j=2)
                    xr = G
                    o_free = [t_yd] * 4
                    prev = rD[1].rearrange("(t p) d -> t p d", p=128)
                    outv = T["out"].rearrange("b (t p) d -> (b t) p d", p=128)
                    for g in range(NT):
                        s = g % 4
                        tx = dma(xr[:, s], prev[g], f"d_xr{s}", o_free[s])
                        for j in range(2):
                            ty = PO.go(lambda e, s=s, j=j, g=g: e.indirect_dma_start(
                                yg[:, s, j, :], None, yD[1], bass.IndirectOffsetOnAxis(ap=dI[:, j, g:g + 1], axis=0)),
                                o_free[s], t_yd, t_dI, sig=S(f"d_yl{s}", 16))
                        x = DV.go(lambda e, s=s, g=g: e.scalar_tensor_tensor(
                            xr[:, s], yg[:, s, 0], w1[:, g:g + 1], xr[:, s], ALU.mult, ALU.add), tx, ty, sig=S("v_fin"))
                        x = DV.go(lambda e, s=s, g=g: e.scalar_tensor_tensor(
                            xr[:, s], yg[:, s, 1], w2[:, g:g + 1], xr[:, s], ALU.mult, ALU.add), x, sig=S("v_fin"))
                        o_free[s] = AC.go(lambda e, s=s, g=g: e.dma_start(outv[g], xr[:, s]), x, sig=S(f"d_out{s}", 16))
                    SP.wait(o_free)
                    AC.wait(o_free)
            ends = [(s, s.n) for n, s in sems.items() if s.n]
            return ends, t_yd

        t_end, t_M = attention(0, None, None)
        t_end, t_yd = experts(0, t_end, t_M, False)
        t_end, t_M = attention(1, t_end, t_yd)
        t_end, t_yd = experts(1, t_end, t_M, True)

        block = ctx.enter_context(nc.Block())

        @block.sync
        def _(e):
            SP.play(e)

        @block.scalar
        def _(e):
            AC.play(e)

        @block.vector
        def _(e):
            DV.play(e)

        @block.gpsimd
        def _(e):
            PO.play(e)

        @block.tensor
        def _(e):
            PE.play(e)


def constants():
    f = np.float32
    cst = np.zeros((128, C_N), f)
    p = np.arange(128)
    cst[:, C_ID:C_ID + 128] = np.eye(128)
    cst[:, C_IOTA:C_IOTA + 128] = p[None, :]
    cst[:, C_TRI:C_TRI + 128] = p[:, None] < p[None, :]
    cst[:, C_P] = p
    cst[:, C_TOK:C_TOK + NT] = np.arange(NT)[None, :] * 128 + p[:, None]
    cst[:, C_I8:C_I8 + 8] = np.arange(8)[None, :]
    start = 2 ** (-2 ** (-(log2(16) - 3)))
    slopes = np.array([start * start ** i for i in range(16)], f)
    c = np.arange(512)
    rel = -np.abs((c[None, :] - 384) - p[:, None]).astype(f)
    seen = (c[None, :] - 384) <= p[:, None]
    alibi = np.where(seen[None], rel[None] * slopes[:, None, None] * f(8), f(-1e30)).astype(f)
    half = 64
    dims = np.arange(half, dtype=f)
    freq = np.power(f(10000.0), -dims / f(half)).astype(f)
    rad = np.arange(N, dtype=f)[:, None] * freq[None, :]
    cos, sin = np.cos(rad).astype(f).T, np.sin(rad).astype(f).T
    rope = np.zeros((128, 3, 512), f)
    rope[:, 0] = np.where(seen, f(0), f(-1e32))
    rope[:, 1] = np.concatenate([cos, cos])
    rope[:, 2] = np.concatenate([sin, -sin])
    return {"c_cst": cst, "c_alibi": np.ascontiguousarray(alibi.transpose(1, 0, 2)), "c_rope": rope}


def kernel(**inputs):
    import numpy as _np
    import concourse.bacc as _bacc
    from concourse import mybir as _mybir
    from concourse.bass_utils import run_bass_kernel_spmd as _run

    g = {k[3:]: _np.asarray(v) for k, v in inputs.items()}

    def rows(w):
        k = w.shape[0] // 128
        return _np.ascontiguousarray(w.reshape(k, 128, -1).transpose(1, 0, 2))

    arrays = dict(constants())
    arrays["x"] = g["attn_a_x"]
    arrays["qkv0"] = rows(g["attn_a_w_qkv"])
    arrays["qkv1"] = rows(_np.concatenate([g[f"attn_b_w_a{n}"].reshape(D, 1024) for n in "qkv"], axis=1))
    arrays["wo0"] = rows(g["attn_a_w_out"])
    arrays["wo1"] = rows(g["attn_b_w_ao"].reshape(1024, D))
    arrays["b_out"] = g["attn_a_b_out"]
    arrays["norm_w"] = g["ffn_norm_w"]
    arrays["gate_wT"] = rows(_np.ascontiguousarray(g["ffn_gate_w"].T))
    arrays["gate_b"] = g["ffn_gate_b"]
    m1 = g["ffn_mlp1_w"].reshape(E, HID, 2, D).transpose(0, 2, 1, 3).reshape(E, 2 * HID, 2, 128)
    arrays["w1"] = _np.ascontiguousarray(m1.transpose(3, 0, 2, 1).reshape(128, E, 4 * HID))
    m2 = g["ffn_mlp2_w"].reshape(E, D, 2, 128)
    arrays["w2"] = _np.ascontiguousarray(m2.transpose(3, 0, 2, 1))
    b1 = g["ffn_mlp1_b"].reshape(E, HID, 2).transpose(0, 2, 1).reshape(-1)
    arrays["mlp_b"] = _np.concatenate([b1, g["ffn_mlp2_b"].reshape(-1)]).reshape(128, 48)

    nc = _bacc.Bacc("TRN2", target_bir_lowering=False, num_devices=1)
    t, feed = {}, {}
    for name, a in arrays.items():
        a = _np.ascontiguousarray(a)
        feed[f"in_{name}"] = a
        t[name] = nc.dram_tensor(f"in_{name}", a.shape, _mybir.dt.from_np(a.dtype), kind="ExternalInput").ap()
    t["out"] = nc.dram_tensor("out_0", (NB, N, D), F32, kind="ExternalOutput").ap()
    t["qkv"] = [t["qkv0"], t["qkv1"]]
    t["wo"] = [t["wo0"], t["wo1"]]
    t["tab"] = [t["c_alibi"], t["c_rope"]]
    program(nc, t)
    r = _run(nc, [feed], core_ids=[0])
    return r.results[0]["out_0"]
```

```python
from contextlib import ExitStack
from math import log2

import numpy as np

import concourse.bass as bass
from concourse import mybir

F32 = mybir.dt.float32
F32R = mybir.dt.float32r
I32 = mybir.dt.int32
U32 = mybir.dt.uint32
ALU = mybir.AluOpType
ACT = mybir.ActivationFunctionType
AX = mybir.AxisListType.X

NB, N, D = 8, 512, 256
TT = N // 128
NT = NB * TT
E, HID = 8, 256
NS = 2 * NT + E - 1
NSP = 72
WIDE = 1280
OFF = [0, 128, 384, 768]
PTO = [0, 512, 1024, 896]
LIMIT, ALPHA = 7.0, 1.702

C_ID, C_IOTA, C_TRI, C_P, C_TOK, C_I8 = 0, 128, 256, 384, 385, 417
C_PAD = 432
C_N = 432 + NSP
PLACES = 2 * NT * 128


class Sem:

    def __init__(self, h, step):
        self.h, self.step, self.n = h, step, 0

    def tick(self):
        self.n += self.step
        return (self, self.n)


class Queue:

    def __init__(self):
        self.items, self.waited = [], {}

    def wait(self, *tokens):
        for t in tokens:
            if t is None:
                continue
            if isinstance(t, list):
                self.wait(*t)
                continue
            s, v = t
            if self.waited.get(id(s), 0) < v:
                self.waited[id(s)] = v
                self.items.append(lambda e, s=s, v=v: e.wait_ge(s.h, v))

    def go(self, fn, *tokens, sig=None):
        self.wait(*tokens)
        if sig is None:
            self.items.append(fn)
            return None
        t = sig.tick()
        self.items.append(lambda e: fn(e).then_inc(sig.h, sig.step))
        return t

    def play(self, e):
        for f in self.items:
            f(e)


def program(nc, T):
    ctx = ExitStack()
    PE, AC, DV, PO, SP = Queue(), Queue(), Queue(), Queue(), Queue()
    sems = {}

    def S(name, step=1):
        if name not in sems:
            sems[name] = Sem(ctx.enter_context(nc.semaphore(name)), step)
        return sems[name]

    def dma(dst, src, name, *tokens):
        return SP.go(lambda e: e.dma_start(dst, src), *tokens, sig=S(name, 16))

    def dram(name, shape):
        return nc.dram_tensor(name, shape, F32).ap()

    with ctx:
        def sb(name, shape, dt=F32, c=ctx):
            return c.enter_context(nc.sbuf_tensor(name, shape, dt))

        bank = [ctx.enter_context(nc.psum_tensor(f"bank{i}", [128, 512], F32)) for i in range(8)]
        hD = [dram(f"hD{i}", [NT * 128, D]) for i in range(2)]
        rD = [dram(f"rD{i}", [NT * 128, D]) for i in range(2)]
        yD = [dram(f"yD{i}", [PLACES + 256, D]) for i in range(2)]

        bD = dram("bD", [2, E * 768])
        cst = sb("cst", [128, C_N])
        ident = cst[:, C_ID:C_ID + 128]
        bout = sb("bout", [128, D])
        nw = sb("nw", [128, D])
        gw = sb("gw", [128, 2, E])
        gb = sb("gb", [128, E])
        mhalf = sb("mhalf", [128, TT])
        stage = sb("stage", [128, 2, 512])
        base = nc.sbuf_base
        with ExitStack() as over:
            Wh = sb("Wh", [128, 2, 3072], F32R, over)
            Wl = sb("Wl", [128, 2, 3072], F32R, over)
        assert nc.sbuf_base == base
        Wraw = sb("Wraw", [128, 12288])
        raw1 = Wraw[:, 0:8192].rearrange("p (x n) -> p x n", x=E)
        raw2 = Wraw[:, 8192:12288]
        WO = sb("WO", [128, 8, D])
        M1 = sb("M1", [128, NT, E])
        M2 = sb("M2", [128, NT, E])
        bh = sb("bh", [128, 48], F32R)
        bl = sb("bl", [128, 48], F32R)
        w1 = sb("w1", [128, NT])
        w2 = sb("w2", [128, NT])
        dI = sb("dI", [128, 2, NT], I32)
        idx = sb("idx", [128, NSP], I32)
        place = sb("place", [128, NSP], I32)
        etab = sb("etab", [1, NSP], I32)

        t_cst = [dma(cst[:], T["c_cst"], "d_cst"), dma(bout[:], T["b_out"].partition_broadcast(128), "d_cst")]
        t_cst = t_cst[-1]
        t_mh = DV.go(lambda e: e.memset(mhalf[:], -0.5), sig=S("v_mh"))
        for q in (PE, AC, DV, PO):
            q.wait(t_cst)
        PO.wait(t_mh)

        def bias_rows():
            braw = stage[:, 0, 0:48]
            t = dma(braw, T["mlp_b"], "d_b0")
            t_bh = AC.go(lambda e: e.copy(bh[:], braw), t, sig=S("a_bh"))
            t_bl = DV.go(lambda e: e.tensor_tensor(bl[:], braw, bh[:].bitcast(F32), ALU.subtract), t_bh, t, sig=S("v_bl"))
            dma(bD[0].rearrange("(p n) -> p n", p=128), bh[:].bitcast(F32), "d_b1", t_bh)
            dma(bD[1].rearrange("(p n) -> p n", p=128), bl[:].bitcast(F32), "d_b1", t_bl)
            return [t_bh, t_bl]

        wsplit, t_raw, wo_free, t_gw = {}, {}, {}, []

        def load_raw(ph, last_proj):
            return [[dma(raw1[:, 4 * i:4 * i + 4], T["w1"][:, 4 * i:4 * i + 4], f"d_raw{ph}{i}", last_proj)
                     for i in range(2)], dma(raw2, T["w2"].rearrange("p x k n -> p (x k n)"), f"d_raw{ph}2", last_proj)]


        def split_weights(ph, slots, free, extra):
            parts = [(c, kc) for c in (0, 2, 4, 1, 3, 5) for kc in range(2)]
            loaded, ns = [], len(slots)

            def load(n):
                c, kc = parts[n]
                loaded.append(dma(slots[n % ns], T["qkv"][ph][:, kc, c * 512:(c + 1) * 512], f"d_st{ph}_{n % ns}",
                                  free[n % ns], extra))

            for n in range(ns):
                load(n)
            yield
            for n, (c, kc) in enumerate(parts):
                k = n % ns
                cs = slice(c * 512, (c + 1) * 512)
                t = loaded[n]
                a = AC.go(lambda e, k=k, kc=kc, cs=cs: e.copy(Wh[:, kc, cs], slots[k]), t, extra, sig=S("a_whi"))
                b = DV.go(lambda e, k=k, kc=kc, cs=cs: e.tensor_tensor(
                    Wl[:, kc, cs], slots[k], Wh[:, kc, cs].bitcast(F32), ALU.subtract), a, t, extra, sig=S("v_wlo"))
                free[k] = [a, b]
                if n + ns < len(parts):
                    load(n + ns)
                wsplit[(ph, c)] = [a, b]
                yield

        def attention(ph, start, t_prev):
            A = ph == 0
            HU = 2 if A else 1
            KD = 64 if A else 128
            NU = NB * 8
            c = ExitStack()

            def b(name, shape, dt=F32):
                return sb(f"{name}_{ph}", shape, dt, c)

            with c:
                tab = b("tab", [128, 16, 512]) if A else b("tab", [128, 3, 512])
                NX = 2 if A else 3
                X = b("X", [128, NX, TT, D])
                xn = b("xn", [128, TT, D])
                xTh = b("xTh", [128, 2, 512], F32R)
                xTl = b("xTl", [128, 2, 512], F32R)
                if A:
                    QS, KS = (b(f"q{i}", [128, 2, 2, 512], F32R) for i in range(2))
                    KL = b("q2", [128, 2, 512], F32R)
                else:
                    Qh, Ql, Kh, Kl = (b(f"q{i}", [128, 2, 512], F32R) for i in range(4))
                V = b("V", [128, 2, TT, 512])
                NP = 3 if A else 2
                P = b("P", [128, NP, WIDE])
                PT = b("PT", [128, 2, WIDE])
                OT = b("OT", [128, 8, 512])
                mx = b("mx", [128, NP, 4])
                nm = b("nm", [128, NP, 4])
                rs = b("rs", [128, NP, 4])
                rc = b("rc", [128, NP, 4])
                sts = b("st", [128, 2, TT, 6])
                mvs = b("mv", [128, 2, TT, 2])
                ves = b("ve", [128, 2, TT])
                rstds = b("rstd", [128, 2, TT])
                xs = b("xs", [128, TT, D])
                hh = b("hh", [128, TT, D])
                hT = stage
                ss = b("ss", [128, TT])
                r2 = b("r2", [128, TT])
                lg = b("lg", [128, TT, E])
                v8 = b("v8", [128, TT, E])
                i8 = b("i8", [128, TT, E], U32)
                if8 = b("if8", [128, TT, E])
                dv = b("dv", [128, TT])
                if A:
                    xl = xn
                else:
                    xl = b("xl", [128, TT, D])
                    rp = b("rp", [128, 2, 2, 512])
                    rf = b("rf", [128, 2, 512])
                    yg = b("yg", [128, 4, 2, D])

                jobs = []
                p_last = [None]

                def pool(fn, *tokens, sig):
                    t = PO.go(fn, p_last[0], *tokens, sig=sig)
                    if A:
                        p_last[0] = t
                    return t

                k0 = dma(X[:, 0], T["x"][0].rearrange("(t p) d -> p t d", p=128), "d_x0") if A else None
                if A:
                    weights = split_weights(0, [OT[:, i] for i in range(8)], [None] * 8, None)
                    next(weights)
                    t_tab = [dma(tab[:, 4 * i:4 * i + 4], T["tab"][ph][:, 4 * i:4 * i + 4], f"d_tab{i}", start)
                             for i in range(4)]
                    dma(nw[:], T["norm_w"].partition_broadcast(128), "d_gw")
                    dma(gw[:], T["gate_wT"], "d_gw")
                    t_gw.append(dma(gb[:], T["gate_b"].partition_broadcast(128), "d_gw"))
                    wo_free[0] = dma(WO[:], T["wo"][0], "d_wo0")
                else:
                    t_tab = []
                t_wo = wo_free[0]
                if start:
                    for q in (PE, AC, DV, PO):
                        q.wait(start)

                t_x, t_xT, xT_used = {}, {}, [None]
                t_q, t_v, qk_used, v_used = {}, {}, {}, {}
                p_ready, p_exp, p_used = {}, {}, {}
                pt_ready, pt_used, ot_used = {}, {}, {}
                bank_free = {i: None for i in range(8)}
                t_y, t_xpre = {}, {}
                B_Q, B_S, B_T, B_O, B_M = (0, 1), (2, 3), (4, 5), 6, 7
                cnt = {"s": 0, "t": 0}

                def tick(n=1):
                    while jobs and n:
                        n -= 1
                        if next(jobs[0], jobs) is jobs:
                            jobs.pop(0)

                def need(what, key):
                    while key not in what:
                        tick()

                def load_x(bt):
                    k = bt % NX
                    free = t_y.get(bt - NX)
                    if A and bt == 0:
                        t_x[bt] = k0
                        return
                    if A:
                        t_x[bt] = dma(X[:, k], T["x"][bt].rearrange("(t p) d -> p t d", p=128), f"d_x{k}", free)
                        return
                    prev = rD[0].rearrange("(b t p) d -> b p t d", p=128, t=TT)
                    tx = dma(X[:, k], prev[bt], f"d_x{k}", free)
                    for t in range(TT):
                        g = bt * TT + t
                        yield
                        a = DV.go(lambda e, k=k, t=t, g=g: e.scalar_tensor_tensor(
                            X[:, k, t], yg[:, t, 0], w1[:, g:g + 1], X[:, k, t], ALU.mult, ALU.add), tx, t_yg[bt],
                            sig=S("v_cb"))
                        yield
                        yf = DV.go(lambda e, k=k, t=t, g=g: e.scalar_tensor_tensor(
                            X[:, k, t], yg[:, t, 1], w2[:, g:g + 1], X[:, k, t], ALU.mult, ALU.add), a, sig=S("v_cb"))
                    yg_free[0] = t_x[bt] = yf

                t_yg, yg_free = {}, [None]

                def load_y(bt):
                    for j in range(2):
                        src = yD[0][(j * NB + bt) * N:(j * NB + bt + 1) * N, :].rearrange("(t p) d -> p t d", p=128)
                        t = dma(yg[:, :, j], src, f"d_yg{j}", yg_free[0], t_prev)
                        t_yg.setdefault(bt, []).append(t)
                        yield

                def norm(w, src, dst, ready, free):
                    st, mv, ve, rstd = sts[:, w], mvs[:, w], ves[:, w], rstds[:, w]
                    ts = None
                    for t in range(TT):
                        ts = DV.go(lambda e, t=t: e.bn_stats(st[:, t], src(t)), ready, sig=S("v_st"))
                        if A or t % 2:
                            yield
                    for t in range(TT):
                        ta = DV.go(lambda e, t=t: e.bn_aggr(mv[:, t], st[:, t]), ts, sig=S("v_ag"))
                    tp = pool(lambda e: e.tensor_scalar(ve, mv[:, :, 1], 1e-5, None, ALU.add), ta, sig=S("p_ve"))
                    tp = pool(lambda e: e.tensor_tensor(rstd, ve, mhalf[:], ALU.pow), tp, sig=S("p_rs"))
                    for _ in range(6 if A else 3):
                        yield
                    for t in range(TT):
                        tn = DV.go(lambda e, t=t: e.tensor_scalar(dst[:, t], src(t), mv[:, t, 0:1], rstd[:, t:t + 1],
                                                                  ALU.subtract, ALU.mult), tp, free, sig=S("v_xn"))
                        if A or t % 2:
                            yield
                    return tn

                t_xn, xn_used, xl_used = {}, [None], [None]

                def pre(bt):
                    k = bt % NX
                    tn = yield from norm(0, lambda t: X[:, k, t], xn, t_x[bt], xn_used[0])
                    t_xpre[bt] = tn
                    if A:
                        for t in range(TT):
                            t_xpre[bt] = pool(lambda e, t=t: e.tensor_tensor(X[:, k, t], X[:, k, t], bout[:], ALU.add),
                                               tn, sig=S("p_xb"))
                    t_xn[bt] = tn

                def transpose4(src, kc, ready):
                    for t in range(TT):
                        tp = PE.go(lambda e, t=t: e.transpose(bank[B_M][:, t * 128:(t + 1) * 128],
                                                             src[:, t, kc * 128:(kc + 1) * 128], ident),
                                   ready, bank_free[B_M], sig=S("m_tr") if t == TT - 1 else None)
                    return tp

                def xpose(bt, kc):
                    need(t_xn, bt)
                    tp = transpose4(xn, kc, t_xn[bt])
                    if kc == 1:
                        xn_used[0] = tp
                    a = AC.go(lambda e: e.copy(xTh[:, kc], bank[B_M][:]), tp, xT_used[0], sig=S("a_xT"))
                    v = DV.go(lambda e: e.tensor_tensor(xTl[:, kc], bank[B_M][:], xTh[:, kc].bitcast(F32),
                                                        ALU.subtract), a, xT_used[0], sig=S("v_xT"))
                    bank_free[B_M] = [v]
                    t_xT[bt] = [a, v]

                def mm3(out, lh, ll, rh, rl, first, last, sig, *tok):
                    PE.go(lambda e: e.matmul(out, lh, rh, start=first, stop=False), *tok)
                    PE.go(lambda e: e.matmul(out, lh, rl, start=False, stop=False))
                    return PE.go(lambda e: e.matmul(out, ll, rh, start=False, stop=last), sig=sig if last else None)

                def proj_v(u, ts4):
                    bt, p = divmod(u, 8)
                    g = u // 4
                    vk = g % 2
                    c0 = 2048 + (p // 4) * 512
                    for t in ts4:
                        bk = bank[B_Q[t % 2]]
                        ts = slice(t * 128, (t + 1) * 128)
                        for kc in range(2):
                            tp = mm3(bk[:], xTh[:, kc, ts], xTl[:, kc, ts], Wh[:, kc, c0:c0 + 512],
                                     Wl[:, kc, c0:c0 + 512], kc == 0, kc == 1, S("m_v"), wsplit[(ph, 4 + p // 4)], t_xT[bt],
                                     bank_free[B_Q[t % 2]])
                        if A:
                            a = DV.go(lambda e, t=t, bk=bk: e.tensor_copy(V[:, vk, t], bk[:]), tp, v_used.get(g - 2),
                                      sig=S("v_v"))
                        else:
                            a = AC.go(lambda e, t=t, bk=bk: e.copy(V[:, vk, t], bk[:]), tp, v_used.get(g - 2),
                                      sig=S("a_v"))
                        bank_free[B_Q[t % 2]] = [a]
                        t_v.setdefault(g, []).append(a)
                    xT_used[0] = tp

                def proj_qk(u, j):
                    bt, p = divmod(u, 8)
                    k = u % 2
                    bk = bank[B_Q[j]]
                    c0 = j * 1024 + p * 128
                    for kc in range(2):
                        tp = mm3(bk[:], Wh[:, kc, c0:c0 + 128], Wl[:, kc, c0:c0 + 128], xTh[:, kc], xTl[:, kc],
                                 kc == 0, kc == 1, S("m_qk"), wsplit[(ph, 2 * j + p // 4)], t_xT[bt], bank_free[B_Q[j]])
                    xT_used[0] = tp
                    used = qk_used.get(u - 2)
                    t_q.setdefault(u, [])
                    if A:
                        for hl in range(2):
                            own, other = (slice(64 * i, 64 * i + 64) for i in (hl, 1 - hl))
                            H = (QS, KS)[j][own, k, hl]
                            a = AC.go(lambda e, H=H, own=own: e.copy(H, bk[own, :]), tp, used, sig=S("a_qk"))
                            if j:
                                t_q[u].append(pool(lambda e, H=H, other=other, hl=hl: e.tensor_copy(
                                    KS[other, k, hl], H.bitcast(F32)), a, used, sig=S("p_kd")))

                            def low(H=H, own=own, other=other, hl=hl, a=a):
                                L = KL[own, k] if j else QS[other, k, hl]
                                v = DV.go(lambda e: e.tensor_tensor(L, bk[own, :], H.bitcast(F32), ALU.subtract), a,
                                          used, sig=S("v_qk"))
                                bank_free[B_Q[j]] = [v]
                                t_q[u].extend([a, v])
                            lows.append(low)
                        return
                    rj = rp[:, j]

                    def rope():
                        DV.go(lambda e: e.tensor_tensor(rj[:, 0], bk[:], tab[:, 1], ALU.mult), tp, t_tab, rope_free[j],
                              sig=S("v_rp"))
                        DV.go(lambda e: e.tensor_tensor(rj[0:64, 1], bk[64:128, :], tab[64:128, 2], ALU.mult),
                              sig=S("v_rp"))
                        v = DV.go(lambda e: e.tensor_tensor(rj[64:128, 1], bk[0:64, :], tab[0:64, 2], ALU.mult),
                                  sig=S("v_rp"))
                        bank_free[B_Q[j]] = [v]
                        g = pool(lambda e: e.tensor_tensor(rf[:, j], rj[:, 0], rj[:, 1], ALU.add), v, rf_free[j],
                                  sig=S("p_rf"))
                        rope_free[j] = rope_done[j] = g
                    rope()

                def proj(u, early=lambda: None):
                    if u % 4 == 0:
                        early()
                        proj_v(u, range(TT))
                    proj_qk(u, 0)
                    tick()
                    if u % 4:
                        early()
                    proj_qk(u, 1)

                rope_done = [None, None]

                def rope_split(u):
                    k = u % 2
                    for j, (H, L) in enumerate(((Qh, Ql), (Kh, Kl))):
                        used = qk_used.get(u - 2)
                        a = AC.go(lambda e, H=H, j=j: e.copy(H[:, k], rf[:, j]), rope_done[j], used, sig=S("a_qk"))
                        l = pool(lambda e, H=H, L=L, j=j: e.tensor_tensor(
                            L[:, k], rf[:, j], H[:, k].bitcast(F32), ALU.subtract), a, used, sig=S("p_lo"))
                        rf_free[j] = [a, l]
                        t_q[u] += [a, l]

                rope_free, rf_free = [None, None], [None, None]

                def scores(h, between=()):
                    between = list(between)
                    u, hl = divmod(h, HU)
                    k = u % 2
                    r = slice(64 * hl, 64 * hl + 64) if A else slice(0, 128)
                    pb = h % NP
                    tb = tab[:, h % 16] if A else tab[:, 0]
                    for t in reversed(range(TT)):
                        s = B_S[cnt["s"] % 2]
                        cnt["s"] += 1
                        w = (t + 1) * 128
                        ts = slice(t * 128, w)
                        if A:
                            PE.go(lambda e, s=s, w=w, ts=ts: e.matmul(bank[s][:, 0:w], QS[:, k, hl, ts], KS[:, k, hl, 0:w],
                                                                      start=True, stop=False), t_q[u], bank_free[s])
                            tp = PE.go(lambda e, s=s, w=w, ts=ts: e.matmul(
                                bank[s][:, 0:w], QS[r, k, hl, ts], KL[r, k, 0:w], start=False, stop=True), sig=S("m_s"))
                        else:
                            tp = mm3(bank[s][:, 0:w], Qh[r, k, ts], Ql[r, k, ts], Kh[r, k, 0:w], Kl[r, k, 0:w],
                                     True, True, S("m_s"), t_q[u], bank_free[s])
                        v = DV.go(lambda e, s=s, w=w, t=t: e.tensor_tensor_reduce(
                            out=P[:, pb, OFF[t]:OFF[t] + w], in0=bank[s][:, 0:w], in1=tb[:, 512 - w:512], scale=1.0,
                            scalar=-3e38, op0=ALU.add, op1=ALU.max, accum_out=mx[:, pb, t:t + 1]),
                            tp, t_tab[h % 16 // 4 if A else 0], p_used.get(h - NP), sig=S("v_mx"))
                        bank_free[s] = [v]
                        if between:
                            between.pop(0)()
                        tick()
                    qk_used[u] = tp
                    sc = 0.125 if A else 1.0 / 128
                    t_nm[h] = DV.go(lambda e: e.tensor_scalar(nm[:, pb], mx[:, pb], -sc, None, ALU.mult), v, sig=S("v_nm"))

                t_nm, lows = {}, []

                def exps(h):
                    pb = h % NP
                    sc = 0.125 if A else 1.0 / 128
                    for t in range(TT):
                        ps = P[:, pb, OFF[t]:OFF[t] + (t + 1) * 128]
                        a = AC.go(lambda e, ps=ps, t=t: e.activation(ps, ps, ACT.Exp, bias=nm[:, pb, t:t + 1], scale=sc,
                                                                     accum_out=rs[:, pb, t:t + 1]), t_nm[h], sig=S("a_exp"))
                    p_exp[h] = a

                def scale(h):
                    pb = h % NP
                    r = DV.go(lambda e: e.reciprocal(rc[:, pb], rs[:, pb]), p_exp[h], sig=S("v_rc"))
                    for t in range(TT):
                        ps = P[:, pb, OFF[t]:OFF[t] + (t + 1) * 128]
                        v = DV.go(lambda e, ps=ps, t=t: e.tensor_scalar(ps, ps, rc[:, pb, t:t + 1], None, ALU.mult),
                                  r, sig=S("v_sc"))
                    p_ready[h] = v

                def flip(h):
                    pb = h % NP
                    pt = h % 2
                    pt_ready[h] = []

                    def part(cs):
                        s = B_T[cnt["t"] % 2]
                        cnt["t"] += 1
                        at = 0
                        for cc in cs:
                            for t in range(cc, TT):
                                lastone = cc == cs[-1] and t == TT - 1
                                tp = PE.go(lambda e, at=at, s=s, t=t, cc=cc: e.transpose(
                                    bank[s][:, at:at + 128], P[:, pb, OFF[t] + cc * 128:OFF[t] + cc * 128 + 128], ident),
                                    p_ready[h], bank_free[s], sig=S("m_t") if lastone else None)
                                at += 128
                        dst = PT[:, pt, PTO[cs[0]]:PTO[cs[0]] + at]
                        x = AC.go(lambda e: e.copy(dst, bank[s][:, 0:at]), tp, pt_used.get(h - 2), sig=S("a_pt"))
                        bank_free[s] = [x]
                        p_used[h] = tp
                        pt_ready[h].append(x)
                    return [lambda cs=cs: part(cs) for cs in ((0,), (1, 3), (2,))]

                def attend(u):
                    bt, p = divmod(u, 8)
                    g = u // 4
                    vk = g % 2
                    o = bank[B_O]
                    for cc in range(TT):
                        for hl in range(HU):
                            h = u * HU + hl
                            col = (u % 4) * 128 + hl * 64
                            w = 512 - cc * 128
                            out = o[64 * hl:64 * hl + 64, cc * 128:512] if A else o[:, cc * 128:512]
                            lastone = cc == TT - 1 and hl == HU - 1
                            tp = PE.go(lambda e, out=out, cc=cc, col=col, h=h, w=w: e.matmul(
                                out, V[:, vk, cc, col:col + KD], PT[:, h % 2, PTO[cc]:PTO[cc] + w],
                                start=cc == 0, stop=cc == TT - 1), pt_ready[h], t_v[g], bank_free[B_O],
                                sig=S("m_o") if lastone else None)
                    for hl in range(HU):
                        pt_used[u * HU + hl] = tp
                    if u % 4 == 3:
                        v_used[g] = tp
                    a = AC.go(lambda e: e.copy(OT[:, p], o[:]), tp, ot_used.get(bt - 1), sig=S("a_o"))
                    bank_free[B_O] = [a]
                    t_ot[(bt, p)] = a

                t_ot = {}
                t_x1 = {}

                def outproj(bt, half):
                    for t2 in range(2):
                        t = half * 2 + t2
                        for ch in range(8):
                            tp = PE.go(lambda e, t=t, t2=t2, ch=ch: e.matmul(
                                bank[B_M][:, t2 * 256:t2 * 256 + 256], OT[:, ch, t * 128:(t + 1) * 128], WO[:, ch],
                                start=ch == 0, stop=ch == 7), t_ot[(bt, ch)], t_wo, bank_free[B_M],
                                sig=S("m_y") if t2 == 1 and ch == 7 else None)
                    if half == 1:
                        ot_used[bt] = tp

                    add_x(bt, half, tp)

                def add_x(bt, half, tp):
                    k = bt % NX
                    v = DV.go(lambda e: e.tensor_tensor(X[:, k, 2 * half:2 * half + 2], bank[B_M][:].rearrange(
                        "p (t d) -> p t d", t=2), X[:, k, 2 * half:2 * half + 2], ALU.add), tp, t_xpre[bt], sig=S("v_x1"))
                    bank_free[B_M] = [v]
                    if half:
                        t_x1[bt] = v

                hold = {"hh": None, "xs": None, "xl": None, "hT": None, "lg": None}
                t_hh = {}

                def gate_norm(bt):
                    k = bt % NX
                    tn = yield from norm(1, lambda t: X[:, k, t], xl, t_x1[bt], (xn_used if A else xl_used)[0])
                    for t in range(TT):
                        ta = AC.go(lambda e, t=t: e.activation(xs[:, t], xl[:, t], ACT.Square,
                                                               accum_out=ss[:, t:t + 1]), tn, hold["xs"], sig=S("a_ss"))
                    tg = pool(lambda e: e.tensor_scalar(ves[:, 1], ss[:], 1.0 / D, float(np.finfo(np.float32).eps),
                                                         ALU.mult, ALU.add), ta, sig=S("p_v2"))
                    tg = pool(lambda e: e.tensor_tensor(r2[:], ves[:, 1], mhalf[:], ALU.pow), tg, sig=S("p_r2"))
                    for _ in range(6 if A else 3):
                        yield
                    yield
                    for t in range(TT):
                        th = DV.go(lambda e, t=t: e.scalar_tensor_tensor(hh[:, t], xl[:, t], r2[:, t:t + 1], nw[:],
                                                                         ALU.mult, ALU.mult), tg, hold["hh"], t_gw, sig=S("v_h"))
                        if A or t % 2:
                            yield
                    tx = pool(lambda e: e.tensor_tensor(xs[:], X[:, k], xl[:], ALU.add), ta, tn, sig=S("p_xs"))
                    (xn_used if A else xl_used)[0] = [th, tx]
                    t_y[bt] = [tx]
                    dh = dma(hD[ph].rearrange("(b t p) d -> b p t d", p=128, t=TT)[bt], hh[:], "d_h", th)
                    dx = dma(rD[ph].rearrange("(b t p) d -> b p t d", p=128, t=TT)[bt], xs[:], "d_r", tx)
                    hold["xs"] = [dx]
                    hold["hh"] = [dh]
                    t_hh[bt] = th

                t_hT = {}

                def gate_flip(bt, kc):
                    need(t_hh, bt)
                    tp = transpose4(hh, kc, t_hh[bt])
                    a = AC.go(lambda e: e.copy(hT[:, kc], bank[B_M][:]), tp, hold["hT"], sig=S("a_hT"))
                    bank_free[B_M] = [a]
                    t_hT[bt] = a
                    if kc == 1:
                        hold["hh"] = hold["hh"] + [tp]

                def gate_top(bt):
                    for t in range(TT):
                        for kc in range(2):
                            tp = PE.go(lambda e, t=t, kc=kc: e.matmul(
                                bank[B_M][:, t * E:(t + 1) * E], hT[:, kc, t * 128:(t + 1) * 128], gw[:, kc],
                                start=kc == 0, stop=kc == 1), t_hT[bt], t_gw, bank_free[B_M],
                                sig=S("m_lg") if t == TT - 1 and kc == 1 else None)
                    hold["hT"] = tp
                    v = DV.go(lambda e: e.tensor_tensor(lg[:], bank[B_M][:, 0:TT * E].rearrange("p (t k) -> p t k", k=E),
                                                        gb[:].rearrange("p (a k) -> p a k", a=1).broadcast_to(
                                                            [128, TT, E]), ALU.add), tp, t_gw, hold["lg"], sig=S("v_lg"))
                    bank_free[B_M] = [v]
                    jobs.insert(0, top(bt, v))

                def top(bt, v):
                    yield
                    for t in range(TT):
                        v1 = DV.go(lambda e, t=t: e.max(v8[:, t], lg[:, t]), v, sig=S("v_m8"))
                    yield
                    for t in range(TT):
                        v2 = DV.go(lambda e, t=t: e.max_index(i8[:, t], v8[:, t], lg[:, t]), v1, sig=S("v_i8"))
                    yield
                    v2 = DV.go(lambda e: e.tensor_copy(if8[:], i8[:]), v2, sig=S("v_if"))
                    v3 = DV.go(lambda e: e.tensor_tensor(dv[:], v8[:, :, 1], v8[:, :, 0], ALU.subtract), v1, sig=S("v_dv"))
                    g0 = bt * TT
                    io = cst[:, C_I8:C_I8 + E].rearrange("p (a k) -> p a k", a=1).broadcast_to([128, TT, E])
                    for j, M in enumerate((M1, M2)):
                        m = DV.go(lambda e, j=j, M=M: e.tensor_tensor(
                            M[:, g0:g0 + TT], io, if8[:, :, j:j + 1].broadcast_to([128, TT, E]), ALU.is_equal),
                            v2, sig=S("v_M"))
                    a = AC.go(lambda e: e.activation(dv[:], dv[:], ACT.Exp), v3, sig=S("a_ev"))
                    yield
                    yield
                    v4 = DV.go(lambda e: e.tensor_scalar(w1[:, g0:g0 + TT], dv[:], 1.0, None, ALU.add), a, sig=S("v_w"))
                    v5 = DV.go(lambda e: e.reciprocal(w1[:, g0:g0 + TT], w1[:, g0:g0 + TT]), v4, sig=S("v_w"))
                    v6 = DV.go(lambda e: e.tensor_tensor(w2[:, g0:g0 + TT], w1[:, g0:g0 + TT], dv[:], ALU.mult), v5,
                               sig=S("v_w"))
                    hold["lg"] = v6
                    t_M[bt] = m
                t_M = {}

                if not A:
                    jobs.append(load_y(0))
                jobs.append(load_x(0))
                jobs.append(pre(0))
                xpose(0, 0)
                xpose(0, 1)
                if A:
                    for _ in range(6):
                        next(weights)
                else:
                    t_tab.append(dma(tab[:], T["tab"][ph], "d_tab", start))
                proj(0)
                if not A:
                    rope_split(0)
                while lows:
                    lows.pop(0)()
                proj(1)
                while lows:
                    lows.pop(0)()
                for h in range(HU):
                    scores(h)
                    exps(h)
                if A:
                    for _ in weights:
                        pass
                    hold["hT"] = bias_rows()
                    proj_qk(2, 0)
                else:
                    rope_split(1)
                for h in range(HU):
                    scale(h)
                PF = 3
                for u in range(NU):
                    bt, p = divmod(u, 8)
                    nx = bt + 1 < NB
                    if A and p == 2 and nx:
                        jobs.append(load_x(bt + 1))
                    if not A and bt >= 1:
                        if p == 0:
                            outproj(bt - 1, 0)
                        elif p == PF + 1:
                            gate_top(bt - 1)
                    for hl in range(HU):
                        h = u * HU + hl
                        n = h + HU
                        more = [lambda: xpose(bt + 1, 1)] if p == 5 and hl == HU - 1 and nx else []
                        if n < NU * HU:
                            fl = flip(h)
                            scores(n, fl[:1] + more + fl[1:])
                        else:
                            for f in flip(h):
                                f()
                        if not A:
                            tick()
                            if u >= 1 and u + 2 < NU:
                                rope_split(u + 2)
                        if n < NU * HU:
                            exps(n)
                        while lows and u % 4 > 1:
                            lows.pop(0)()
                        if A and HU <= n - 1 < NU * HU:
                            scale(n - 1)
                        while lows:
                            lows.pop(0)()
                        if A and u + 2 + hl < NU:
                            proj_qk(u + 2 + hl, 1 - hl)
                        if A and u % 4 > 1 and u // 4 * 4 + 4 < NU:
                            proj_v(u // 4 * 4 + 4, (2 * (u % 4 - 2) + hl,))
                        if A and p == 5 and hl == 0 and nx:
                            xpose(bt + 1, 0)
                        if A and p == 0 and bt >= 1:
                            outproj(bt - 1, hl)
                        if A and p == PF and bt >= 1 and hl == 0:
                            gate_flip(bt - 1, 0)
                    if not A and p == 0 and bt >= 1:
                        outproj(bt - 1, 1)
                    if p == 0 and bt >= 1:
                        jobs.insert(0, gate_norm(bt - 1))
                    if not A and u == 0:
                        jobs += [load_y(1), load_x(1), pre(1)]
                    if not A and bt >= 1 and p == PF:
                        gate_flip(bt - 1, 0)
                    if u == 0 and not A:
                        proj(2)
                        rope_split(2)
                    early = (lambda: scale(n)) if not A and n < NU * HU else (lambda: None)
                    if A:
                        pass
                    elif u + 3 < NU:
                        proj(u + 3, early)
                    else:
                        early()
                    if bt >= 1:
                        if p == PF:
                            gate_flip(bt - 1, 1)
                        elif A and p == PF + 1:
                            gate_top(bt - 1)
                    if A and p == 2 and nx:
                        jobs.append(pre(bt + 1))
                    if u == (NU - 3 if A else NU - 4):
                        t_raw[ph] = load_raw(ph, xT_used[0])
                    if A:
                        tick()
                    attend(u)
                    tick()
                    if not A and p == 4 and nx:
                        xpose(bt + 1, 0)
                    if not A and p == 5 and bt + 2 < NB:
                        jobs += [load_y(bt + 2), load_x(bt + 2), pre(bt + 2)]
                bt = NB - 1
                outproj(bt, 0)
                outproj(bt, 1)
                jobs.append(gate_norm(bt))
                gate_flip(bt, 0)
                gate_flip(bt, 1)
                gate_top(bt)
                need(t_M, bt)
                t_M = t_M[bt]
            ends = [S(n) for n in sems if n[0] in "mavpd"]
            return [(s, s.n) for s in ends if s.n], t_M

        def experts(ph, t_end, t_M, last):
            c = ExitStack()

            def b(name, shape, dt=F32):
                return sb(f"{name}f_{ph}", shape, dt, c)

            with c:
                W1h = b("W1h", [128, E, 2, 512], F32R)
                W1l = b("W1l", [128, E, 2, 512], F32R)
                W2 = b("W2", [128, E, 2, D])
                BR = b("BR", [2, E * 768], F32R)
                on2 = b("on2", [2, 128], F32R)
                Ms = b("Ms", [128, NT, E])
                Tt = b("Tt", [128, NT, E])
                inc = b("inc", [128, NT, E])
                tmp = b("tmp", [128, NT, E])
                tm2 = b("tm2", [128, NT, E])
                one = b("one", [128, NT])
                n8 = b("n8", [128, 4, E])
                ni = b("ni", [128, E], I32)
                dF = b("dF", [128, 2, NT])
                ia = b("ia", [128, 2, NT], I32)
                fa = b("fa", [128, 2, NT])
                fb = b("fb", [128, 2, NT])
                nf = b("nf", [128, 2, NT])
                ls = b("ls", [128, NSP])
                pl = b("pl", [128, 2, NSP])
                ntok = b("ntok", [128, NT])
                ob = b("ob", [128, 6, 128], F32R)
                oa = b("oa", [128, 6, NSP], F32R)
                se = b("se", [1, NSP, E])
                ef = b("ef", [1, NSP])
                G = b("G", [128, 4, D])
                ab = G[:].rearrange("p s (h n) -> p (s h) n", n=128)
                XTh = b("XTh", [128, 2, 2, 128], F32R)
                XTl = b("XTl", [128, 2, 2, 128], F32R)
                gl = b("gl", [128, 2, HID])
                li = b("li", [128, 2, HID])
                sg = b("sg", [128, 2, HID])
                ac = b("ac", [128, 2, HID])
                AT = b("AT", [128, 2, 2, 128])
                Y = b("Y", [128, 2, D])
                for q in (PE, AC, DV, PO, SP):
                    q.wait(t_end)

                v = DV.go(lambda e: e.tensor_tensor(Ms[:], M1[:], M2[:], ALU.add), t_M, sig=S("r_v"))
                flat = Ms[:].rearrange("p t k -> p (t k)")
                ones = b("ones", [128, 128])
                vo = DV.go(lambda e: e.memset(ones[:], 1.0), sig=S("r_v"))
                t_nt = DV.go(lambda e: e.tensor_scalar(ntok[:], cst[:, C_TOK:C_TOK + NT], -1.0, None, ALU.mult),
                             sig=S("r_v"))
                von = DV.go(lambda e: e.memset(one[:], 1.0), sig=S("r_v"))
                PE.go(lambda e: e.matmul(bank[0][:, 0:256], cst[:, C_TRI:C_TRI + 128], flat, start=True, stop=True), v, vo)
                t_rk = PE.go(lambda e: e.matmul(bank[1][:, 0:256], ones[:], flat, start=True, stop=True), sig=S("r_m"))
                v = DV.go(lambda e: e.tensor_copy(Tt[:].rearrange("p t k -> p (t k)"), bank[1][:, 0:256]), t_rk, sig=S("r_v"))
                for k in range(E):
                    vs = DV.go(lambda e, k=k: e.tensor_tensor_scan(inc[:, :, k], one[:], Tt[:, :, k], 0.0,
                                                                  ALU.mult, ALU.add), v, von, sig=S("r_v"))
                v1 = DV.go(lambda e: e.tensor_scalar(n8[:, 0], inc[:, NT - 1], 127.0, None, ALU.add), vs, sig=S("r_v"))
                v1 = DV.go(lambda e: e.tensor_copy(ni[:], n8[:, 0]), v1, sig=S("r_v"))
                v1 = DV.go(lambda e: e.tensor_single_scalar(ni[:], ni[:], 7, ALU.arith_shift_right), v1, sig=S("r_v"))
                v1 = DV.go(lambda e: e.tensor_copy(n8[:, 1], ni[:]), v1, sig=S("r_v"))
                v1 = DV.go(lambda e: e.tensor_tensor_scan(n8[:, 2], one[:, 0:E], n8[:, 1], 0.0, ALU.mult, ALU.add), v1,
                           sig=S("r_v"))
                t_inc = v1
                v1 = DV.go(lambda e: e.tensor_tensor(n8[:, 3], n8[:, 2], n8[:, 1], ALU.subtract), v1, sig=S("r_v"))
                v1 = DV.go(lambda e: e.tensor_scalar(n8[:, 3], n8[:, 3], 128.0, None, ALU.mult), v1, sig=S("r_v"))
                v2 = DV.go(lambda e: e.tensor_tensor(tmp[:], inc[:], Tt[:], ALU.subtract), vs, sig=S("r_v"))
                v2 = DV.go(lambda e: e.tensor_tensor(tmp[:].rearrange("p t k -> p (t k)"), bank[0][:, 0:256],
                                                     tmp[:].rearrange("p t k -> p (t k)"), ALU.add), v2, sig=S("r_v"))
                v2 = DV.go(lambda e: e.tensor_tensor(tmp[:], tmp[:], n8[:, 3:4].broadcast_to([128, NT, E]), ALU.add),
                           v2, v1, sig=S("r_v"))
                for j, M in enumerate((M1, M2)):
                    v3 = DV.go(lambda e, M=M: e.tensor_tensor(tm2[:], M[:], tmp[:], ALU.mult), v2, sig=S("r_v"))
                    v2 = DV.go(lambda e, j=j: e.reduce_sum(dF[:, j], tm2[:], AX), v3, sig=S("r_v"))
                v2 = DV.go(lambda e: e.tensor_copy(dI[:], dF[:]), v2, sig=S("r_v"))
                v2 = DV.go(lambda e: e.tensor_single_scalar(ia[:], dI[:], 7, ALU.arith_shift_right), v2, sig=S("r_v"))
                v2 = DV.go(lambda e: e.tensor_copy(fa[:], ia[:]), v2, sig=S("r_v"))
                v2 = DV.go(lambda e: e.scalar_tensor_tensor(fb[:], fa[:], -128.0, dF[:], ALU.mult, ALU.add), v2, sig=S("r_v"))
                tbr = dma(BR[:].bitcast(F32), bD, "d_BR")
                von2 = DV.go(lambda e: e.tensor_copy(on2[:], ones[0:2, :]), vo, sig=S("r_v"))
                raw, raw_w2 = t_raw[ph]
                tw = []
                for k in range(E):
                    W1f = [w[:, k].rearrange("p a b -> p (a b)") for w in (W1h, W1l)]
                    a = AC.go(lambda e, k=k, W1f=W1f: e.copy(W1f[0], raw1[:, k]), raw[k // 4], sig=S("a_w1"))
                    g = PO.go(lambda e, k=k, W1f=W1f: e.tensor_tensor(W1f[1], raw1[:, k], W1f[0].bitcast(F32),
                                                                    ALU.subtract), a, raw[k // 4], sig=S("p_w1"))
                    tw = [a, g]

                t_fb = DV.go(lambda e: e.tensor_scalar(nf[:], fb[:], -1.0, None, ALU.mult), v2, sig=S("r_v"))
                ob_free, ab_used, n1, nj = [None] * 6, {}, 0, [0, 0]
                tokc = [cst[:, C_TOK + t:C_TOK + t + 1] for t in range(NT)]

                def collect(j, x, y):
                    nonlocal n1
                    k, m = n1 % 6, nj[j]
                    nj[j] += 1
                    ob_free[k] = PE.go(lambda e: e.matmul(bank[2 + j][:, 0:NSP], ob[:, k], oa[:, k], start=m == 0,
                                                          stop=m == NT - 1), x, y, sig=S("r_id"))
                    n1 += 1

                def by_scalar(g, t_ab):
                    t, j = divmod(g, 2)
                    k, a = n1 % 6, g // 2 % 8
                    x = AC.go(lambda e: e.activation(ob[:, k], ab[:, a], ACT.Relu, scale=ntok[:, t:t + 1], bias=tokc[t]),
                              t_ab, t_nt, ob_free[k], sig=S("r_oc"))
                    ab_used[a] = x
                    y = DV.go(lambda e: e.tensor_scalar(oa[:, k], cst[:, C_IOTA:C_IOTA + NSP], fa[:, j, t:t + 1], None,
                                                        ALU.is_equal), v2, ob_free[k], sig=S("r_oa"))
                    collect(j, x, y)

                def by_vector(g):
                    t, j = divmod(g, 2)
                    k = n1 % 6
                    x = DV.go(lambda e: e.tensor_scalar(ob[:, k], cst[:, C_IOTA:C_IOTA + 128], fb[:, j, t:t + 1], None,
                                                        ALU.is_equal), v2, ob_free[k], sig=S("r_ob"))
                    y = DV.go(lambda e: e.tensor_scalar(oa[:, k], cst[:, C_IOTA:C_IOTA + NSP], fa[:, j, t:t + 1], tokc[t],
                                                        ALU.is_equal, ALU.mult), v2, ob_free[k], sig=S("r_oa"))
                    collect(j, x, y)

                held = None
                for g in range(2 * NT):
                    if g % 2 == 0:
                        by_vector(g)
                        continue
                    t, j = divmod(g, 2)
                    a = g // 2 % 8
                    x = AC.go(lambda e, a=a, t=t, j=j: e.activation(ab[:, a], cst[:, C_IOTA:C_IOTA + 128], ACT.Abs,
                                                                    bias=nf[:, j, t:t + 1]), t_fb, ab_used.get(a),
                              sig=S("r_ab"))
                    if held:
                        by_scalar(*held)
                    held = (g, x)
                by_scalar(*held)
                last_id = ob_free[(n1 - 1) % 6]
                t_ls = DV.go(lambda e: e.tensor_copy(ls[:], bank[2][:, 0:NSP]), last_id, sig=S("r_v"))
                t_ls = DV.go(lambda e: e.tensor_tensor(ls[:], bank[3][:, 0:NSP], ls[:], ALU.add), t_ls, sig=S("r_v"))
                t_idx = DV.go(lambda e: e.tensor_scalar(idx[:], ls[:], -1.0, 0.0, ALU.add, ALU.max), t_ls, sig=S("r_v"))
                vp = DV.go(lambda e: e.tensor_scalar(pl[:, 0], bank[3][:, 0:NSP], 0.0, float(NT * 128), ALU.is_gt,
                                                     ALU.mult), last_id, sig=S("r_v"))
                vq = DV.go(lambda e: e.scalar_tensor_tensor(pl[:, 1], ls[:], 0.0, cst[:, C_PAD:C_PAD + NSP], ALU.is_equal,
                                                            ALU.mult), t_ls, sig=S("r_v"))
                vp = DV.go(lambda e: e.tensor_tensor(pl[:, 0], pl[:, 0], ls[:], ALU.add), vp, sig=S("r_v"))
                t_place = DV.go(lambda e: e.scalar_tensor_tensor(place[:], pl[:, 0], -1.0, pl[:, 1], ALU.add, ALU.add),
                                vp, vq, sig=S("r_v"))

                v4 = DV.go(lambda e: e.tensor_tensor(
                    se[:], cst[0:1, C_IOTA:C_IOTA + NSP].rearrange("p (s a) -> p s a", a=1).broadcast_to([1, NSP, E]),
                    n8[0:1, 2:3, :].broadcast_to([1, NSP, E]), ALU.is_ge), t_inc, sig=S("r_v"))
                v4 = DV.go(lambda e: e.reduce_sum(ef[:], se[:], AX), v4, sig=S("r_v"))
                v4 = DV.go(lambda e: e.tensor_scalar(ef[:], ef[:], float(E - 1), None, ALU.min), v4, sig=S("r_v"))
                t_et = DV.go(lambda e: e.tensor_copy(etab[:], ef[:]), v4, sig=S("r_v"))

                tw2 = dma(W2[:].rearrange("p x k n -> p (x k n)"), raw2, "d_w2", raw_w2)
                more = iter(()) if last else split_weights(1, [stage[:, i] for i in range(2)], [t_end, t_end], [tw, tw2])

                g_free, t_g = {}, {}
                xt_free, t_xt = {}, {}
                gl_free, t_ac = {}, {}
                at_free, y_free = {}, {}
                bf = {i: [t_idx, t_place] for i in range(8)}
                B1, BX, BA, BY = (0, 1), (2, 3), (4, 5), (6, 7)
                t_yd = []

                def gather(a):
                    t_g[a] = PO.go(lambda e: e.indirect_dma_start(G[:, a % 4], None, hD[ph], bass.IndirectOffsetOnAxis(
                        ap=idx[:, a:a + 1], axis=0)), t_idx, g_free.get(a - 4), sig=S(f"d_g{a % 4}", 16))

                def flip_x(a):
                    k = a % 2
                    bk = bank[BX[k]]
                    for kc in range(2):
                        tp = PE.go(lambda e, kc=kc: e.transpose(bk[:, kc * 128:(kc + 1) * 128],
                                                               G[:, a % 4, kc * 128:(kc + 1) * 128], ident),
                                   t_g[a], bf[BX[k]], sig=S("f_x") if kc else None)
                    g_free[a] = tp
                    src = bk[:, 0:256].rearrange("p (a b) -> p a b", a=2)
                    x = AC.go(lambda e: e.copy(XTh[:, k], src), tp, xt_free.get(a - 2), sig=S("a_fx"))
                    y = DV.go(lambda e: e.tensor_tensor(XTl[:, k], src, XTh[:, k].bitcast(F32), ALU.subtract), x,
                              xt_free.get(a - 2), sig=S("v_fx"))
                    bf[BX[k]] = [y]
                    t_xt[a] = [x, y]

                def up(a):
                    k = a % 2
                    bk = bank[B1[k]]
                    PE.wait(t_et, tw, tbr, von2, t_xt[a], bf[B1[k]])

                    def f(e):
                        r = e.value_load(etab[0:1, a:a + 1], min_val=0, max_val=E - 1)
                        ex = bass.ds(r, 1)
                        bias = BR[:, 0:E * 512].rearrange("q (x n) -> q x n", x=E)
                        e.matmul(bk[:], on2[:], bias[:, ex].rearrange("q x n -> q (x n)"), start=True, stop=False)
                        for kc in range(2):
                            wh = W1h[:, ex, kc].rearrange("p x n -> p (x n)")
                            wl = W1l[:, ex, kc].rearrange("p x n -> p (x n)")
                            e.matmul(bk[:], XTh[:, k, kc], wh, start=False, stop=False)
                            e.matmul(bk[:], XTh[:, k, kc], wl, start=False, stop=False)
                            i = e.matmul(bk[:], XTl[:, k, kc], wh, start=False, stop=kc == 1)
                        return i
                    tp = PE.go(f, sig=S("f_up"))
                    xt_free[a] = tp
                    g = DV.go(lambda e: e.tensor_scalar(gl[:, k], bk[:, 0:HID], LIMIT, None, ALU.min), tp, gl_free.get(a - 2),
                              sig=S("v_gl"))
                    s = AC.go(lambda e: e.activation(sg[:, k], gl[:, k], ACT.Sigmoid, scale=ALPHA), g, gl_free.get(a - 2),
                              sig=S("a_sg"))
                    l = DV.go(lambda e: e.tensor_scalar(li[:, k], bk[:, HID:2 * HID], LIMIT, -LIMIT, ALU.min, ALU.max), tp,
                              gl_free.get(a - 2), sig=S("v_li"))
                    bf[B1[k]] = [l]
                    m = DV.go(lambda e: e.scalar_tensor_tensor(li[:, k], li[:, k], 1.0, gl[:, k], ALU.add, ALU.mult), l, g,
                              sig=S("v_lg2"))
                    m = DV.go(lambda e: e.tensor_tensor(ac[:, k], li[:, k], sg[:, k], ALU.mult), m, s, at_free.get(a - 2),
                              sig=S("v_ac"))
                    gl_free[a] = m
                    t_ac[a] = m

                t_at, t_xr = {}, {}

                def flip_a(a):
                    k = a % 2
                    bk = bank[BA[k]]
                    for kc in range(2):
                        tp = PE.go(lambda e, kc=kc: e.transpose(bk[:, kc * 128:(kc + 1) * 128],
                                                               ac[:, k, kc * 128:(kc + 1) * 128], ident),
                                   t_ac[a], bf[BA[k]], sig=S("f_a") if kc else None)
                    at_free[a] = tp
                    src = bk[:, 0:256].rearrange("p (a b) -> p a b", a=2)
                    x = AC.go(lambda e: e.copy(AT[:, k], src), tp, t_dn.get(a - 2), sig=S("a_at"))
                    bf[BA[k]] = [x]
                    t_at[a] = x

                t_dn = {}

                def down(a):
                    k = a % 2
                    bk = bank[BY[k]]
                    PE.wait(tw2, t_at[a], bf[BY[k]])

                    def f(e):
                        r = e.value_load(etab[0:1, a:a + 1], min_val=0, max_val=E - 1)
                        ex = bass.ds(r, 1)
                        bias = BR[:, E * 512:E * 768].rearrange("q (x n) -> q x n", x=E)
                        e.matmul(bk[:, 0:D], on2[:], bias[:, ex].rearrange("q x n -> q (x n)"), start=True, stop=False)
                        for kc in range(2):
                            i = e.matmul(bk[:, 0:D], AT[:, k, kc], W2[:, ex, kc].rearrange("p x n -> p (x n)"),
                                         start=False, stop=kc == 1)
                        return i
                    tp = PE.go(f, sig=S("f_dn"))
                    t_dn[a] = tp
                    x = AC.go(lambda e: e.copy(Y[:, k], bk[:, 0:D]), tp, y_free.get(a - 2), sig=S("a_y"))
                    bf[BY[k]] = [x]
                    y_free[a] = PO.go(lambda e: e.indirect_dma_start(
                        yD[ph], bass.IndirectOffsetOnAxis(ap=place[:, a:a + 1], axis=0), Y[:, k], None), x, t_place,
                        sig=S(f"d_y{k}", 16))

                for a in range(4):
                    gather(a)
                flip_x(0)
                flip_x(1)
                up(0)
                up(1)
                flip_x(2)
                gather(4)
                gather(5)
                for a in range(NS):
                    flip_a(a)
                    if a % 4 == 3:
                        next(more, None)
                    if a == 20 and last:
                        for bt in range(NB):
                            t_xr[bt] = dma(Wraw[:, bt * 1024:(bt + 1) * 1024].rearrange("p (t d) -> p t d", t=TT),
                                           rD[1].rearrange("(b t p) d -> b p t d", p=128, t=TT)[bt], f"d_xr{bt}", tw)
                    if a == 52 and not last:
                        wo_free[0] = dma(WO[:], T["wo"][1], "d_wo1")
                    if a + 3 < NS:
                        flip_x(a + 3)
                    if a + 6 < NS:
                        gather(a + 6)
                    if a + 2 < NS:
                        up(a + 2)
                    down(a)
                t_yd = [y_free[NS - 1], y_free[NS - 2]]

                if last:
                    xr = Wraw[:, 0:8192].rearrange("p (b t d) -> p b t d", b=NB, t=TT)
                    rooms = [Wraw[:, 8192:10240], Wraw[:, 10240:12288]]
                    for w in (W1h, W1l):
                        wide = w[:].bitcast(F32).rearrange("p x k n -> p (x k n)")
                        rooms += [wide[:, i * 2048:(i + 1) * 2048] for i in range(3)]
                    rooms = [m.rearrange("p (j t d) -> p j t d", j=2, t=TT) for m in rooms]
                    outv = T["out"].rearrange("b (t p) d -> b p t d", p=128)
                    t_y1, o_free = {}, []
                    for bt in range(NB):
                        for j in (1, 0):
                            src = yD[1][(j * NB + bt) * N:(j * NB + bt + 1) * N, :].rearrange("(t p) d -> p t d", p=128)
                            t_y1[(bt, j)] = dma(rooms[bt][:, j], src, f"d_yl{j}{bt}", t_yd, xt_free[NS - 1])
                    for bt in range(NB):
                        y0, y1 = rooms[bt][:, 0], rooms[bt][:, 1]
                        for t in range(TT):
                            g = bt * TT + t
                            a = AC.go(lambda e, g=g, t=t, y1=y1: e.activation(y1[:, t], y1[:, t], ACT.Copy,
                                                                              scale=w2[:, g:g + 1]), t_y1[(bt, 1)],
                                      sig=S("a_fin"))
                        for t in range(TT):
                            g = bt * TT + t
                            x = DV.go(lambda e, g=g, t=t, y0=y0, bt=bt: e.scalar_tensor_tensor(
                                xr[:, bt, t], y0[:, t], w1[:, g:g + 1], xr[:, bt, t], ALU.mult, ALU.add), t_xr[bt],
                                t_y1[(bt, 0)], sig=S("v_fin"))
                        x = DV.go(lambda e, y1=y1, bt=bt: e.tensor_tensor(xr[:, bt], xr[:, bt], y1, ALU.add), a, x,
                                  sig=S("v_fin"))
                        o_free.append(dma(outv[bt], xr[:, bt], f"d_out{bt}", x))
                    SP.wait(o_free)
                    AC.wait(o_free)
            ends = [(s, s.n) for n, s in sems.items() if s.n]
            return ends, t_yd

        t_end, t_M = attention(0, None, None)
        t_end, t_yd = experts(0, t_end, t_M, False)
        t_end, t_M = attention(1, t_end, t_yd)
        t_end, t_yd = experts(1, t_end, t_M, True)

        block = ctx.enter_context(nc.Block())

        @block.sync
        def _(e):
            SP.play(e)

        @block.scalar
        def _(e):
            AC.play(e)

        @block.vector
        def _(e):
            DV.play(e)

        @block.gpsimd
        def _(e):
            PO.play(e)

        @block.tensor
        def _(e):
            PE.play(e)


def constants():
    f = np.float32
    cst = np.zeros((128, C_N), f)
    p = np.arange(128)
    cst[:, C_ID:C_ID + 128] = np.eye(128)
    cst[:, C_IOTA:C_IOTA + 128] = p[None, :]
    cst[:, C_TRI:C_TRI + 128] = p[:, None] < p[None, :]
    cst[:, C_P] = p
    cst[:, C_TOK:C_TOK + NT] = np.arange(NT)[None, :] * 128 + p[:, None] + 1
    cst[:, C_I8:C_I8 + 8] = np.arange(8)[None, :]
    cst[:, C_PAD:C_PAD + NSP] = PLACES + 1 + p[:, None] + 128 * (np.arange(NSP)[None, :] % 2)
    start = 2 ** (-2 ** (-(log2(16) - 3)))
    slopes = np.array([start * start ** i for i in range(16)], f)
    c = np.arange(512)
    rel = -np.abs((c[None, :] - 384) - p[:, None]).astype(f)
    seen = (c[None, :] - 384) <= p[:, None]
    alibi = np.where(seen[None], rel[None] * slopes[:, None, None] * f(8), f(-1e30)).astype(f)
    half = 64
    dims = np.arange(half, dtype=f)
    freq = np.power(f(10000.0), -dims / f(half)).astype(f)
    rad = np.arange(N, dtype=f)[:, None] * freq[None, :]
    cos, sin = np.cos(rad).astype(f).T, np.sin(rad).astype(f).T
    rope = np.zeros((128, 3, 512), f)
    rope[:, 0] = np.where(seen, f(0), f(-1e32))
    rope[:, 1] = np.concatenate([cos, cos])
    rope[:, 2] = np.concatenate([sin, -sin])
    return {"c_cst": cst, "c_alibi": np.ascontiguousarray(alibi.transpose(1, 0, 2)), "c_rope": rope}


def kernel(**inputs):
    import numpy as _np
    import concourse.bacc as _bacc
    from concourse import mybir as _mybir
    from concourse.bass_utils import run_bass_kernel_spmd as _run

    g = {k[3:]: _np.asarray(v) for k, v in inputs.items()}

    def rows(w):
        k = w.shape[0] // 128
        return _np.ascontiguousarray(w.reshape(k, 128, -1).transpose(1, 0, 2))

    arrays = dict(constants())
    arrays["x"] = g["attn_a_x"]
    arrays["qkv0"] = rows(g["attn_a_w_qkv"])
    arrays["qkv1"] = rows(_np.concatenate([g[f"attn_b_w_a{n}"].reshape(D, 1024) for n in "qkv"], axis=1))
    arrays["wo0"] = rows(g["attn_a_w_out"])
    arrays["wo1"] = rows(g["attn_b_w_ao"].reshape(1024, D))
    arrays["b_out"] = g["attn_a_b_out"]
    arrays["norm_w"] = g["ffn_norm_w"]
    arrays["gate_wT"] = rows(_np.ascontiguousarray(g["ffn_gate_w"].T))
    arrays["gate_b"] = g["ffn_gate_b"]
    m1 = g["ffn_mlp1_w"].reshape(E, HID, 2, D).transpose(0, 2, 1, 3).reshape(E, 2 * HID, 2, 128)
    arrays["w1"] = _np.ascontiguousarray(m1.transpose(3, 0, 2, 1).reshape(128, E, 4 * HID))
    m2 = g["ffn_mlp2_w"].reshape(E, D, 2, 128)
    arrays["w2"] = _np.ascontiguousarray(m2.transpose(3, 0, 2, 1))
    b1 = g["ffn_mlp1_b"].reshape(E, HID, 2).transpose(0, 2, 1).reshape(-1)
    arrays["mlp_b"] = _np.concatenate([b1, g["ffn_mlp2_b"].reshape(-1)]).reshape(128, 48)

    nc = _bacc.Bacc("TRN2", target_bir_lowering=False, num_devices=1)
    t, feed = {}, {}
    for name, a in arrays.items():
        a = _np.ascontiguousarray(a)
        feed[f"in_{name}"] = a
        t[name] = nc.dram_tensor(f"in_{name}", a.shape, _mybir.dt.from_np(a.dtype), kind="ExternalInput").ap()
    t["out"] = nc.dram_tensor("out_0", (NB, N, D), F32, kind="ExternalOutput").ap()
    t["qkv"] = [t["qkv0"], t["qkv1"]]
    t["wo"] = [t["wo0"], t["wo1"]]
    t["tab"] = [t["c_alibi"], t["c_rope"]]
    program(nc, t)
    r = _run(nc, [feed], core_ids=[0])
    return r.results[0]["out_0"]
```
